# Optimizing a Trainium2 kernel written in Bass

```python
import numpy as np
import jax
import jax.numpy as jnp

def _softmax(x, axis=-1):
    return jax.nn.softmax(x, axis=axis)

def _gelu(x):
    return jax.nn.gelu(x, approximate=True)

def _silu(x):
    return jax.nn.silu(x)

def _sigmoid(x):
    return jax.nn.sigmoid(x)

def _layernorm(x, axis=-1, eps=1e-05):
    m = jnp.mean(x, axis=axis, keepdims=True)
    v = jnp.var(x, axis=axis, keepdims=True)
    return (x - m) / jnp.sqrt(v + eps)

def _scatter_add(tgt, idx, src, axis=0):
    return tgt.at[idx].add(src)

def _segment_sum(src, seg, n):
    return jax.ops.segment_sum(src, seg, n)
kernel_name = 'mk_gnn_preln_d1_gnn_r8_cec065'

def setup_inputs(seed: int=0):
    np.random.seed(seed)
    _w = jnp.asarray

    def _rec_inputs():
        import jax
        import jax.numpy as jnp
        _gk = jax.random.key(seed)
        x = -0.0003713 + 1 * jax.random.normal(jax.random.fold_in(_gk, 1), (6250, 256), jnp.float32)
        src = jax.random.randint(jax.random.fold_in(_gk, 2), (100000,), 0, 6250, jnp.int32)
        dst = jnp.minimum((6250 * jax.random.uniform(jax.random.fold_in(_gk, 3), (100000,)) ** 2.0).astype(jnp.int32), 49999)
        _o = jnp.argsort(dst, stable=True)
        src = src[_o]
        dst = dst[_o]
        edge_weight = jax.random.uniform(jax.random.fold_in(_gk, 12), (100000,), jnp.float32, 0.0, 9.99998)
        return (x, src, dst, edge_weight)
    x, src, dst, edge_weight = _rec_inputs()

    def _L0_gnn_setup():
        import jax, jax.numpy as jnp
        import numpy as np
        CUTOFF = 10.0
        EPS_W = 1e-05
        EPS_LN = 1e-05

        def _silu(v):
            return v * jax.nn.sigmoid(v)
        key = jax.random.key(seed)
        ks = jax.random.split(key, 12)
        N, E, H, R = (6250, 37500, 256, 64)
        s = lambda fan_in: 1.0 / np.sqrt(fan_in)
        inp = {'x': jax.random.normal(ks[0], (N, H), jnp.float32), 'edge_index': jax.random.randint(ks[1], (2, E), 0, N, jnp.int64 if jax.config.jax_enable_x64 else jnp.int32), 'distances': jax.random.uniform(ks[2], (E,), jnp.float32) * CUTOFF, 'centers': jnp.linspace(0.0, CUTOFF, R).astype(jnp.float32), 'widths': jnp.full((R,), CUTOFF / R, jnp.float32), 'rbf_w1': jax.random.normal(ks[3], (R, R), jnp.float32) * s(R), 'rbf_b1': jnp.zeros((R,), jnp.float32), 'rbf_w2': jax.random.normal(ks[4], (R, R), jnp.float32) * s(R), 'rbf_b2': jnp.zeros((R,), jnp.float32), 'filt_w1': jax.random.normal(ks[5], (R, H), jnp.float32) * s(R), 'filt_b1': jnp.zeros((H,), jnp.float32), 'filt_w2': jax.random.normal(ks[6], (H, H), jnp.float32) * s(H), 'filt_b2': jnp.zeros((H,), jnp.float32), 'filt_w3': jax.random.normal(ks[7], (H, H), jnp.float32) * s(H), 'filt_b3': jnp.zeros((H,), jnp.float32), 'node_w': jax.random.normal(ks[8], (H, H), jnp.float32) * s(H), 'node_b': jnp.zeros((H,), jnp.float32), 'ln_g': jnp.ones((H,), jnp.float32), 'ln_b': jnp.zeros((H,), jnp.float32), 'gate_w': jax.random.normal(ks[9], (H, H), jnp.float32) * s(H), 'gate_b': jnp.zeros((H,), jnp.float32)}
        return inp
    _L0_gnn_all = _L0_gnn_setup()
    _L0_gnn_in = {k: v for k, v in _L0_gnn_all.items() if k in ('centers', 'widths', 'rbf_w1', 'rbf_b1', 'rbf_w2', 'rbf_b2', 'filt_w1', 'filt_b1', 'filt_w2', 'filt_b2', 'filt_w3', 'filt_b3', 'node_w', 'node_b', 'ln_g', 'ln_b', 'gate_w', 'gate_b')}
    del _L0_gnn_all
    return {'x': x, 'src': src, 'dst': dst, 'edge_weight': edge_weight, 'L0_gnn_centers': _L0_gnn_in['centers'], 'L0_gnn_widths': _L0_gnn_in['widths'], 'L0_gnn_rbf_w1': _L0_gnn_in['rbf_w1'], 'L0_gnn_rbf_b1': _L0_gnn_in['rbf_b1'], 'L0_gnn_rbf_w2': _L0_gnn_in['rbf_w2'], 'L0_gnn_rbf_b2': _L0_gnn_in['rbf_b2'], 'L0_gnn_filt_w1': _L0_gnn_in['filt_w1'], 'L0_gnn_filt_b1': _L0_gnn_in['filt_b1'], 'L0_gnn_filt_w2': _L0_gnn_in['filt_w2'], 'L0_gnn_filt_b2': _L0_gnn_in['filt_b2'], 'L0_gnn_filt_w3': _L0_gnn_in['filt_w3'], 'L0_gnn_filt_b3': _L0_gnn_in['filt_b3'], 'L0_gnn_node_w': _L0_gnn_in['node_w'], 'L0_gnn_node_b': _L0_gnn_in['node_b'], 'L0_gnn_ln_g': _L0_gnn_in['ln_g'], 'L0_gnn_ln_b': _L0_gnn_in['ln_b'], 'L0_gnn_gate_w': _L0_gnn_in['gate_w'], 'L0_gnn_gate_b': _L0_gnn_in['gate_b']}

def reference(x, src, dst, edge_weight, L0_gnn_centers, L0_gnn_widths, L0_gnn_rbf_w1, L0_gnn_rbf_b1, L0_gnn_rbf_w2, L0_gnn_rbf_b2, L0_gnn_filt_w1, L0_gnn_filt_b1, L0_gnn_filt_w2, L0_gnn_filt_b2, L0_gnn_filt_w3, L0_gnn_filt_b3, L0_gnn_node_w, L0_gnn_node_b, L0_gnn_ln_g, L0_gnn_ln_b, L0_gnn_gate_w, L0_gnn_gate_b):
    import jax
    import jax.numpy as jnp

    def _L0_gnn_ref(x, edge_index, distances, centers, widths, rbf_w1, rbf_b1, rbf_w2, rbf_b2, filt_w1, filt_b1, filt_w2, filt_b2, filt_w3, filt_b3, node_w, node_b, ln_g, ln_b, gate_w, gate_b):
        import jax, jax.numpy as jnp
        import numpy as np
        CUTOFF = 10.0
        EPS_W = 1e-05
        EPS_LN = 1e-05

        def _silu(v):
            return v * jax.nn.sigmoid(v)
        d = distances
        env = 0.5 * (jnp.cos(d * jnp.pi / CUTOFF) + 1.0) * (d < CUTOFF).astype(x.dtype)
        rbf = jnp.exp(-0.5 * ((d[:, None] - centers) / (jnp.abs(widths) + EPS_W)) ** 2)
        r = rbf * env[:, None]
        r = _silu(r @ rbf_w1 + rbf_b1) @ rbf_w2 + rbf_b2
        W = _silu(r @ filt_w1 + filt_b1)
        W = _silu(W @ filt_w2 + filt_b2) @ filt_w3 + filt_b3
        row, col = (edge_index[0], edge_index[1])
        msg = (x[col] @ node_w + node_b) * W
        agg = jax.ops.segment_sum(msg, row, num_segments=x.shape[0])
        h = x + agg
        mu = jnp.mean(h, axis=-1, keepdims=True)
        var = jnp.var(h, axis=-1, keepdims=True)
        out = (h - mu) / jnp.sqrt(var + EPS_LN) * ln_g + ln_b
        return out * jax.nn.sigmoid(out @ gate_w + gate_b)
    edge_index = jnp.stack([src, dst])
    h = jnp.maximum(_layernorm(x, axis=-1), 0.0)
    x = x + _L0_gnn_ref(h, edge_index, edge_weight, L0_gnn_centers, L0_gnn_widths, L0_gnn_rbf_w1, L0_gnn_rbf_b1, L0_gnn_rbf_w2, L0_gnn_rbf_b2, L0_gnn_filt_w1, L0_gnn_filt_b1, L0_gnn_filt_w2, L0_gnn_filt_b2, L0_gnn_filt_w3, L0_gnn_filt_b3, L0_gnn_node_w, L0_gnn_node_b, L0_gnn_ln_g, L0_gnn_ln_b, L0_gnn_gate_w, L0_gnn_gate_b)
    return x

_drawn_inputs = setup_inputs


def setup_inputs(seed=0):
    import zlib

    import numpy as np

    out = dict(_drawn_inputs(seed))
    spreads = {'L0_gnn_widths': (0.15625, 0.6),
     'L0_gnn_rbf_b1': (0.0, 0.297),
     'L0_gnn_rbf_b2': (0.0, 0.1),
     'L0_gnn_filt_b1': (0.0, 0.1),
     'L0_gnn_filt_b2': (0.0, 0.1),
     'L0_gnn_filt_b3': (0.0, 0.1),
     'L0_gnn_node_b': (0.0, 0.1),
     'L0_gnn_ln_g': (1.0, 0.2),
     'L0_gnn_ln_b': (0.0, 0.1),
     'L0_gnn_gate_b': (0.0, 0.546)}
    factors = {'edge_weight': 44.0, 'L0_gnn_centers': 42.603, 'L0_gnn_rbf_w1': 40.888}
    for name, (base, spread) in spreads.items():
        noise = np.random.default_rng([zlib.crc32(name.encode()), seed]).standard_normal(out[name].shape)
        drawn = base * np.exp(spread * noise) if base else spread * noise
        out[name] = jnp.asarray(drawn.astype(out[name].dtype))
    for name, factor in factors.items():
        out[name] = (out[name] * factor).astype(out[name].dtype)
    return out
```

```python
from contextlib import ExitStack

import numpy as np

import concourse.bass as bass
from concourse import mybir

P = 128
HID = 256
R = 64
N_NODES = 6250
N_EDGES = 100000

G_T = 5
G_ROWS = G_T * P
N_GROUPS = 10
N_PAD = N_GROUPS * G_ROWS
DUMP = N_PAD
T_ROWS = N_PAD + P

TILE = P
CHUNK = 4 * TILE
SUPER = 2 * CHUNK
N_SUPER = -(-N_EDGES // SUPER)
N_SUPER += N_SUPER % 2
N_CHUNK = 2 * N_SUPER
E_PAD = N_SUPER * SUPER
E_COLS = E_PAD // P
N_TAB = 2

CUTOFF = 10.0
EPS_W = 1e-05
EPS_LN = 1e-05
ROUND = 1.5 * 2.0 ** 23

F32 = mybir.dt.float32
BF16 = mybir.dt.bfloat16
I32 = mybir.dt.int32
ALU = mybir.AluOpType
ACT = mybir.ActivationFunctionType
AX_X = mybir.AxisListType.X


def build(nc, x, src_cols, src_rows, dst_cols, dist, centers, widths, w1, b1, w2t, b2, f1, fb1,
          f2, fb2, f3, fb3, node_w, node_b, ln_g, ln_b, gate_w, gate_b, out):
    with ExitStack() as ctx:
        def sb(name, shape, dt=F32):
            return ctx.enter_context(nc.sbuf_tensor(name, shape, dt))

        def ps(name):
            return ctx.enter_context(nc.psum_tensor(name, [P, 512], F32))

        def sem(name):
            return ctx.enter_context(nc.semaphore(name))

        hn_tab = nc.dram_tensor("hn_tab", [N_PAD, HID], F32).ap()
        agg = [nc.dram_tensor(f"agg{i}", [T_ROWS, HID], F32).ap() for i in range(N_TAB)]
        env_d = nc.dram_tensor("env_d", [E_PAD], F32).ap()

        w1_sb = sb("w1_sb", [P, P])
        w2t_sb = sb("w2t_sb", [R, P])
        f1_sb = sb("f1_sb", [R, HID])
        w23_sb = sb("w23_sb", [P, HID])
        f2_sb = sb("f2_sb", [P, 2, HID])
        f3_sb = sb("f3_sb", [P, 2, HID])
        nw_sb = sb("nw_sb", [P, 2, HID])
        gw_sb = sb("gw_sb", [P, 2, HID])
        b1_sb = sb("b1_sb", [P, 1])
        b2_sb = sb("b2_sb", [R, 1])
        fb1_sb = sb("fb1_sb", [P, 2])
        b23_sb = sb("b23_sb", [P, 2])
        fb2_sb = sb("fb2_sb", [P, 2])
        b3_rows = sb("b3_rows", [96, 3, HID])
        b3_bf = sb("b3_bf", [96, 3, HID], BF16)
        b3_parts = sb("b3_parts", [96, HID], BF16)
        ones_bf = sb("ones_bf", [96, P], BF16)
        nb_bc = sb("nb_bc", [P, HID])
        lg_bc = sb("lg_bc", [P, HID])
        lb_bc = sb("lb_bc", [P, HID])
        gb_bc = sb("gb_bc", [P, HID])
        cen_sb = sb("cen_sb", [P, 1])
        wid_sb = sb("wid_sb", [P, 1])
        rw_sb = sb("rw_sb", [P, 1])
        ident = sb("ident", [P, P])
        lower = sb("lower", [P, P])
        dump_i = sb("dump_i", [P, 1], I32)
        dump_f = sb("dump_f", [P, 1])
        half_pi = sb("half_pi", [P, 1])
        dist_c = sb("dist_c", [P, E_COLS])
        ev = [sb(f"ev{i}", [P, E_COLS]) for i in range(3)]

        xg = [sb(f"xg{i}", [P, G_T, HID]) for i in range(2)]
        hg = [sb(f"hg{i}", [P, G_T, HID]) for i in range(2)]
        og = [sb(f"og{i}", [P, G_T, HID]) for i in range(2)]
        hT = [sb(f"hT{i}", [P, G_T, 2, P]) for i in range(2)]
        st6 = sb("st6", [P, G_T, 6])
        st2 = [sb(f"st2{i}", [P, G_T, 2]) for i in range(2)]
        var_e = sb("var_e", [P, G_T])
        seed = sb("seed", [P, G_T], I32)
        yy = sb("yy", [P, G_T])
        rstd = [sb(f"rstd{i}", [P, G_T]) for i in range(4)]
        tab = [[sb(f"tab{i}{k}", [P, G_T, HID]) for k in range(N_TAB)] for i in range(2)]

        d_bc = [sb(f"d_bc{i}", [P, CHUNK]) for i in range(2)]
        e_bc = [sb(f"e_bc{i}", [P, CHUNK]) for i in range(2)]
        src_r = [sb(f"src_r{i}", [P, SUPER], I32) for i in range(2)]
        src_c = [sb(f"src_c{i}", [P, 8], I32) for i in range(2)]
        dst_c = [sb(f"dst_c{i}", [P, 8], I32) for i in range(2)]
        u = [sb(f"u{i}", [P, CHUNK]) for i in range(2)]
        usq = [sb(f"usq{i}", [P, CHUNK]) for i in range(2)]
        rbf = [sb(f"rbf{i}", [P, CHUNK]) for i in range(2)]
        r_in = [sb(f"r_in{i}", [P, CHUNK]) for i in range(2)]
        a1 = [sb(f"a1{i}", [P, CHUNK]) for i in range(2)]
        same = [sb(f"same{i}", [P, 8, P]) for i in range(2)]
        same_lo = sb("same_lo", [P, 8, P])
        n_before = sb("n_before", [P, 8])
        is_dup = sb("is_dup", [P, 8])
        to_dump = sb("to_dump", [P, 8])
        src_f = sb("src_f", [P, 8])
        target = [sb(f"target{i}", [P, 8], I32) for i in range(2)]
        hn_g = [[sb(f"hn_g{i}_{j}", [P, 2, HID]) for j in range(4)] for i in range(2)]
        summed = [[sb(f"summed{i}_{j}", [P, 2, HID]) for j in range(4)] for i in range(2)]
        a2 = [sb(f"a2{i}", [P, 2, CHUNK]) for i in range(2)]
        a3 = [sb(f"a3{i}", [P, 2, CHUNK]) for i in range(2)]
        msg = [[sb(f"msg{i}_{j}", [P, 2, HID]) for j in range(2)] for i in range(2)]

        z1 = ps("z1")
        z2 = [ps("z2a"), ps("z2b")]
        z3 = [ps("z3a"), ps("z3b")]
        wps = [ps("wa"), ps("wb")]
        cps = ps("cps")

        w1_clear = sem("w1_clear")
        wts_in = sem("wts_in")
        bc_in = sem("bc_in")
        dist_in = sem("dist_in")
        p_step = sem("p_step")
        pool_pass = sem("pool_pass")
        ve_pass = sem("ve_pass")
        p_const = sem("p_const")
        x_in = [sem("x_in0"), sem("x_in1")]
        hn_out = [sem("hn_out0"), sem("hn_out1")]
        h_out = [sem("h_out0"), sem("h_out1")]
        zeroed = sem("zeroed")
        v_env = sem("v_env")
        a_env = sem("a_env")
        env_ok = sem("env_ok")
        env_out = sem("env_out")
        fuse_mm = sem("fuse_mm")
        fuse_v = sem("fuse_v")
        b3_step = sem("b3_step")
        v_small = sem("v_small")
        ln_step = sem("ln_step")
        h_ready = sem("h_ready")
        t_ready = sem("t_ready")
        hT_ready = sem("hT_ready")
        np_ready = sem("np_ready")
        hn_ready = sem("hn_ready")
        tab_in = [sem("tab_in0"), sem("tab_in1")]
        fn_ready = sem("fn_ready")
        ft_ready = sem("ft_ready")
        fnT_ready = sem("fnT_ready")
        gp_ready = sem("gp_ready")
        gz_ready = sem("gz_ready")
        sg_ready = sem("sg_ready")
        fg_ready = sem("fg_ready")
        out_ready = sem("out_ready")
        out_st = [sem("out_st0"), sem("out_st1")]

        d_in = [sem("d_in0"), sem("d_in1")]
        idx_in = [sem("idx_in0"), sem("idx_in1")]
        gath = [[sem(f"gath{i}_{j}") for j in range(4)] for i in range(2)]
        scat = [sem(f"scat{i}") for i in range(N_TAB)]
        u_ready = sem("u_ready")
        sq_ready = sem("sq_ready")
        exp_ready = sem("exp_ready")
        r_ready = sem("r_ready")
        z1_ready = sem("z1_ready")
        a1_ready = sem("a1_ready")
        z2_ready = sem("z2_ready")
        a2_ready = sem("a2_ready")
        z3_ready = sem("z3_ready")
        a3_ready = sem("a3_ready")
        w_ready = sem("w_ready")
        msg_ready = sem("msg_ready")
        same_ready = sem("same_ready")
        lo_ready = sem("lo_ready")
        cnt_ready = sem("cnt_ready")
        dup_ready = sem("dup_ready")
        dump_ready = sem("dump_ready")
        tgt_ready = sem("tgt_ready")
        c_ready = sem("c_ready")
        sum_ready = sem("sum_ready")

        N_WTS = 17
        N_BC = 4
        LN_STEPS = 14
        x_v = x.rearrange("(g p t) h -> g p t h", p=P, t=G_T)
        out_v = out.rearrange("(g p t) h -> g p t h", p=P, t=G_T)
        hn_v = hn_tab.rearrange("(g p t) h -> g p t h", p=P, t=G_T)
        agg_v = [a[0:N_PAD, :].rearrange("(g p t) h -> g p t h", p=P, t=G_T) for a in agg]
        dist_ch = dist.rearrange("(c a e) -> c a e", a=1, e=CHUNK)
        env_ch = env_d.rearrange("(c a e) -> c a e", a=1, e=CHUNK)
        srow_v = src_rows.rearrange("(s a e) -> s a e", a=1, e=SUPER)

        def row(v, n=P):
            return v.rearrange("(a n) -> a n", a=1).to_broadcast([n, v.shape[0]])

        def col(v):
            return v.rearrange("(n a) -> n a", a=1)

        def per_tile(v, n=G_T):
            return v[:].rearrange("p (a h) -> p a h", a=1).to_broadcast([P, n, HID])

        def count(engine, semaphore, n):
            if not isinstance(n, int) or n > 0:
                engine.wait_ge(semaphore, n)

        def node_loop(eng, step, extra):
            for g in range(2):
                step(g, g // 2, g % 2)
            with eng.Fori(1, N_GROUPS // 2) as it:
                for half in range(2):
                    step(it * 2 + half, it, half)
            for g in range(N_GROUPS, N_GROUPS + extra):
                step(g, g // 2, g % 2)

        def edge_loop(eng, step, extra):
            for t in range(8):
                step(t, t // 4, t % 4)
            with eng.Fori(2, N_CHUNK // 4 - 1) as it:
                for k in range(4):
                    step(it * 4 + k, it, k)
            for t in range(N_CHUNK - 4, N_CHUNK + extra):
                step(t, t // 4, t % 4)

        def exists(c, last=N_CHUNK):
            return not isinstance(c, int) or 0 <= c < last

        block = ctx.enter_context(nc.Block())

        @block.sync
        def _(sp):
            sp.dma_start(dist_c[:], dist.rearrange("(p c) -> p c", p=P)).then_inc(dist_in, 16)

            def weights():
                for dst, src in ((nb_bc[:], node_b), (lg_bc[:], ln_g), (lb_bc[:], ln_b), (gb_bc[:], gate_b)):
                    sp.dma_start(dst, row(src)).then_inc(bc_in, 16)
                sp.wait_ge(w1_clear, 1)
                for dst, src in ((w1_sb[0:R, 0:R], w1), (w1_sb[R:P, R:P], w1),
                                 (w2t_sb[:], w2t), (f1_sb[:], f1),
                                 (f2_sb[:], f2.rearrange("(k p) n -> p k n", p=P)),
                                 (f3_sb[:], f3.rearrange("(k p) n -> p k n", p=P)),
                                 (nw_sb[:], node_w.rearrange("(k p) n -> p k n", p=P)),
                                 (gw_sb[:], gate_w.rearrange("(k p) n -> p k n", p=P)),
                                 (b1_sb[0:R, :], col(b1)), (b1_sb[R:P, :], col(b1)),
                                 (b2_sb[:], col(b2)),
                                 (fb1_sb[:], fb1), (fb2_sb[:], fb2),
                                 (b3_rows[:, 0, :], row(fb3, 96)),
                                 (cen_sb[0:R, :], col(centers)), (cen_sb[R:P, :], col(centers)),
                                 (wid_sb[:], widths)):
                    sp.dma_start(dst, src).then_inc(wts_in, 16)

            def nodes(g, n, half):
                if exists(g, N_GROUPS):
                    count(sp, h_ready, g - 1)
                    sp.dma_start(xg[half][:], x_v[g]).then_inc(x_in[half], 16)
                if isinstance(g, int) and g == 0:
                    weights()
                if exists(g - 1, N_GROUPS):
                    sp.wait_ge(h_ready, g)
                    sp.dma_start(agg_v[0][g - 1], hg[1 - half][:]).then_inc(h_out[1 - half], 16)
                if exists(g - 2, N_GROUPS):
                    sp.wait_ge(hn_ready, g - 1)
                    sp.dma_start(hn_v[g - 2], og[half][:]).then_inc(hn_out[half], 16)

            node_loop(sp, nodes, 2)

            sp.wait_ge(env_ok, 1)
            sp.dma_start(env_d.rearrange("(p c) -> p c", p=P), ev[0][:]).then_inc(env_out, 16)
            sp.wait_ge(env_out, 16)

            def distances(s, q):
                count(sp, r_ready, s - 1)
                for half in range(2):
                    part = slice(half * R, half * R + R)
                    sp.dma_start(d_bc[q][part, :], dist_ch[s * 2 + half].to_broadcast([R, CHUNK])).then_inc(d_in[q], 16)
                    sp.dma_start(e_bc[q][part, :], env_ch[s * 2 + half].to_broadcast([R, CHUNK])).then_inc(d_in[q], 16)

            def indices(s, q):
                count(sp, tgt_ready, s - 1)
                count(sp, msg_ready, s * 4 - 4)
                sp.dma_start(src_r[q][:], srow_v[s].to_broadcast([P, SUPER])).then_inc(idx_in[q], 16)
                sp.dma_start(src_c[q][:], src_cols[s]).then_inc(idx_in[q], 16)
                sp.dma_start(dst_c[q][:], dst_cols[s]).then_inc(idx_in[q], 16)

            def two(n):
                for q in range(2):
                    distances(n * 2 + q, q)
                if not isinstance(n, int) or n > 0:
                    indices(n * 2 - 1, 1)
                indices(n * 2, 0)

            for n in range(2):
                two(n)
            with sp.Fori(2, N_SUPER // 2) as it:
                two(it)
            indices(N_SUPER - 1, 1)

            for i in range(N_TAB):
                sp.wait_ge(scat[i], 16 * N_SUPER * 8 // N_TAB)

            def last(g, n, half):
                if exists(g, N_GROUPS):
                    count(sp, out_ready, g - 1)
                    for i in range(N_TAB):
                        sp.dma_start(tab[half][i][:], agg_v[i][g]).then_inc(tab_in[half], 16)
                    sp.dma_start(xg[half][:], x_v[g]).then_inc(tab_in[half], 16)
                if exists(g - 1, N_GROUPS):
                    sp.wait_ge(out_ready, g)
                    sp.dma_start(out_v[g - 1], og[1 - half][:]).then_inc(out_st[1 - half], 16)

            node_loop(sp, last, 1)
            for half in range(2):
                sp.wait_ge(out_st[half], 16 * N_GROUPS // 2)

        @block.gpsimd
        def _(pool):
            pool.memset(w1_sb[:], 0.0).then_inc(w1_clear, 1)
            pool.memset(ident[:], 0.0).then_inc(p_step, 1)
            pool.memset(lower[:], 1.0).then_inc(p_step, 1)
            pool.iota(dump_i[:], pattern=[[0, 1]], base=DUMP, channel_multiplier=1).then_inc(p_step, 1)
            for i in range(N_TAB):
                pool.memset(tab[0][i][:], 0.0).then_inc(p_step, 1)
            pool.wait_ge(p_step, 3 + N_TAB)
            pool.affine_select(out=ident[:], in_=ident[:], compare_op=ALU.not_equal, fill=1.0,
                               base=0, pattern=[[-1, P]], channel_multiplier=1).then_inc(p_const, 1)
            pool.affine_select(out=lower[:], in_=lower[:], compare_op=ALU.is_gt, fill=0.0,
                               base=0, pattern=[[-1, P]], channel_multiplier=1).then_inc(p_const, 1)
            n_zero = 0
            for i in range(N_TAB):
                pool.dma_start(agg[i][DUMP:T_ROWS, :], tab[0][i][:, 0, :]).then_inc(zeroed, 16)
                n_zero += 1
            for i in range(1, N_TAB):
                for g in range(N_GROUPS):
                    pool.dma_start(agg_v[i][g], tab[0][i][:]).then_inc(zeroed, 16)
                    n_zero += 1

            for half in range(2):
                pool.wait_ge(hn_out[half], 16 * N_GROUPS // 2)

            def gather(s, n, q, j):
                pool.indirect_dma_start(
                    out=hn_g[q][j // 2][:, j % 2, :], out_offset=None, in_=hn_tab,
                    in_offset=bass.IndirectOffsetOnAxis(ap=dst_c[q][:, j:j + 1], axis=0),
                ).then_inc(gath[q][j // 2], 16)

            def scatter(s, n, q, j):
                i = j % N_TAB
                per = 8 // N_TAB
                if j % 2 == 0:
                    pool.wait_ge(sum_ready, s * 4 + j // 2 + 1)
                if j == 0:
                    pool.wait_ge(tgt_ready, s + 1)
                count(pool, scat[i], (s * per + j // N_TAB) * 16)
                if not isinstance(s, int):
                    pool.sem_inc(pool_pass, 1)
                pool.indirect_dma_start(
                    out=agg[i], out_offset=bass.IndirectOffsetOnAxis(ap=target[q][:, j:j + 1], axis=0),
                    in_=summed[q][j // 2][:, j % 2, :], in_offset=None, compute_op=ALU.add,
                ).then_inc(scat[i], 16)

            def superchunk(s, n, q):
                if exists(s, N_SUPER):
                    pool.wait_ge(idx_in[q], 48 * (n + 1))
                if isinstance(s, int) and s == 2:
                    for half in range(2):
                        pool.wait_ge(h_out[half], 16 * N_GROUPS // 2)
                    pool.wait_ge(zeroed, 16 * n_zero)
                for j in range(8):
                    if exists(s, N_SUPER):
                        if j % 2 == 0:
                            count(pool, msg_ready, s * 4 - 8 + j // 2 + 1)
                            if not isinstance(s, int):
                                pool.sem_inc(pool_pass, 1)
                        gather(s, n, q, j)
                    if exists(s - 2, N_SUPER):
                        scatter(s - 2, n - 1, q, j)

            for s in range(4):
                superchunk(s, s // 2, s % 2)
            with pool.Fori(2, N_SUPER // 2) as it:
                for q in range(2):
                    superchunk(it * 2 + q, it, q)
            for s in range(N_SUPER, N_SUPER + 2):
                superchunk(s, s // 2, s % 2)

        @block.scalar
        def _(act):
            def transposed(g, half, ready, prev_used, done):
                act.wait_ge(ready, g + 1)
                count(act, prev_used, g - 1)
                flat = hT[half][:].rearrange("p t k n -> p (t k n)")
                for b, bank in enumerate((z1, z2[0], z2[1])):
                    n = min(512, G_T * HID - 512 * b)
                    i = act.activation(flat[:, 512 * b:512 * b + n], bank[:, 0:n], ACT.Copy)
                i.then_inc(done, 1)

            act.wait_ge(v_small, 1)
            act.wait_ge(v_env, 4)
            act.activation(ev[1][:], ev[0][:], ACT.Sin, bias=half_pi[:], scale=-2.0 * np.pi).then_inc(a_env, 1)

            node_loop(act, lambda g, n, half: transposed(g, half, t_ready, np_ready, hT_ready), 0)

            def squares(s, q):
                act.wait_ge(u_ready, s + 1)
                act.activation(usq[q][:], u[q][:], ACT.Square).then_inc(sq_ready, 1)

            def exps(s, q):
                act.wait_ge(sq_ready, s + 1)
                count(act, r_ready, s - 1)
                act.activation(rbf[q][:], usq[q][:], ACT.Exp, scale=-0.5).then_inc(exp_ready, 1)

            def silu1(s, q):
                act.wait_ge(z1_ready, s + 1)
                count(act, z2_ready, s * 4 - 4)
                act.activation(a1[q][:], z1[:], ACT.Silu, bias=b1_sb[:]).then_inc(a1_ready, 1)

            def step(t, n, k):
                if exists(t):
                    for m in range(2):
                        act.wait_ge(z2_ready, t * 2 + m + 1)
                        if m == 0:
                            count(act, z3_ready, t * 2 - 2)
                        act.activation(a2[k % 2][:, m, :], z2[m][:], ACT.Silu, bias=b23_sb[:, m:m + 1]).then_inc(a2_ready, 1)
                c = t - 3
                q = ((k + 1) // 2) % 2

                def take_sums(pair):
                    if exists(c):
                        act.wait_ge(c_ready, c * 2 + pair + 1)
                        h = (k + 1) % 2
                        slot = 2 * h + pair
                        for i in range(N_TAB):
                            count(act, scat[i], (c * 2 + pair - 7) * (32 // N_TAB))
                        act.activation(summed[q][slot][:].rearrange("p a h -> p (a h)"), cps[:], ACT.Copy).then_inc(sum_ready, 1)

                take_sums(0)
                if exists(t - 1):
                    for m in range(2):
                        act.wait_ge(z3_ready, (t - 1) * 2 + m + 1)
                        if m == 0:
                            count(act, w_ready, t * 2 - 4)
                        act.activation(a3[(k + 1) % 2][:, m, :], z3[m][:], ACT.Silu, bias=fb2_sb[:, m:m + 1]).then_inc(a3_ready, 1)
                take_sums(1)
                if k % 2 == 1:
                    s = n * 2 + (k + 1) // 2
                    if exists(s, N_SUPER):
                        silu1(s, (k + 1) // 2 % 2)
                if k == 2 and exists(n * 2 + 2, N_SUPER):
                    for i in range(2):
                        squares(n * 2 + 2 + i, i)
                    for i in range(2):
                        exps(n * 2 + 2 + i, i)

            for q in range(2):
                squares(q, q)
            for q in range(2):
                exps(q, q)
            silu1(0, 0)
            edge_loop(act, step, 3)

            def last(g, n, half):
                if exists(g, N_GROUPS):
                    transposed(g, half, ft_ready, gp_ready, fnT_ready)
                    act.wait_ge(gz_ready, g + 1)
                    act.activation(tab[half][0][:], og[half][:], ACT.Sigmoid).then_inc(sg_ready, 1)

            node_loop(act, last, 0)

        @block.tensor
        def _(pe):
            pe.wait_ge(wts_in, 16 * N_WTS)
            nc.tensor.matmul(z3[0][:, 0:HID], w2t_sb[:], f1_sb[:], start=True, stop=True)
            for m in range(2):
                i = nc.tensor.matmul(z3[1][:, m:m + 1], f1_sb[:, m * P:(m + 1) * P], b2_sb[:], start=True, stop=True)
            i.then_inc(fuse_mm, 1)

            pe.wait_ge(p_const, 2)
            pe.wait_ge(fuse_v, 2)

            def group(g, src, half, ready, tr, trT, prod, prod_used, w):
                pe.wait_ge(ready, g + 1)
                count(pe, trT, g)
                for x_ in range(2 * G_T):
                    bank = (z1, z2[0], z2[1])[x_ // 4]
                    i = nc.tensor.transpose(bank[:, (x_ % 4) * P:(x_ % 4 + 1) * P],
                                            src[half][:, x_ // 2, (x_ % 2) * P:(x_ % 2 + 1) * P], ident[:])
                i.then_inc(tr, 1)
                pe.wait_ge(trT, g + 1)
                count(pe, prod_used, g)
                for t in range(G_T):
                    bank = (z3[0], z3[1], wps[0])[t // 2]
                    for kk in range(2):
                        i = nc.tensor.matmul(bank[:, (t % 2) * HID:(t % 2 + 1) * HID], hT[half][:, t, kk, :], w[:, kk, :],
                                             start=kk == 0, stop=kk == 1)
                i.then_inc(prod, 1)

            node_loop(pe, lambda g, n, half: group(g, hg, half, h_ready, t_ready, hT_ready, np_ready, hn_ready, nw_sb), 0)

            def layer1(s, q):
                pe.wait_ge(r_ready, s + 1)
                if isinstance(s, int) and s == 0:
                    pe.wait_ge(hT_ready, N_GROUPS)
                count(pe, a1_ready, s)
                nc.tensor.matmul(z1[:], w1_sb[:], r_in[q][:], start=True, stop=True).then_inc(z1_ready, 1)

            def step(t, n, k):
                if exists(t):
                    h = k % 2
                    part = slice(h * R, h * R + R)
                    q = k // 2
                    if h == 0:
                        pe.wait_ge(a1_ready, n * 2 + q + 1)
                    for m in range(2):
                        count(pe, a2_ready, t * 2 - 1 + m)
                        nc.tensor.matmul(z2[m][:], w23_sb[part, m * P:(m + 1) * P], a1[q][part, :],
                                         start=True, stop=True).then_inc(z2_ready, 1)
                c = t - 3
                q3 = ((k + 1) // 2) % 2
                h3 = (k + 1) % 2

                def add_equal(pair):
                    if not exists(c):
                        return
                    pe.wait_ge(msg_ready, c * 2 + pair + 1)
                    if pair == 0 and h3 == 0:
                        pe.wait_ge(same_ready, n * 2 + (k + 1) // 2 - 1)
                    count(pe, sum_ready, c * 2 + pair)
                    for i2 in range(2):
                        i = nc.tensor.matmul(cps[:, i2 * HID:(i2 + 1) * HID], same[q3][:, h3 * 4 + pair * 2 + i2, :],
                                             msg[h3][pair][:, i2, :], start=True, stop=True)
                    i.then_inc(c_ready, 1)

                add_equal(0)
                if exists(t - 1):
                    c1 = (k + 1) % 2
                    pe.wait_ge(a2_ready, t * 2)
                    for m in range(2):
                        count(pe, a3_ready, t * 2 - 3 + m)
                        for kk in range(2):
                            i = nc.tensor.matmul(z3[m][:], f2_sb[:, kk, m * P:(m + 1) * P], a2[c1][:, kk, :],
                                                 start=kk == 0, stop=kk == 1)
                        i.then_inc(z3_ready, 1)
                add_equal(1)
                if exists(t - 2):
                    c2 = k % 2
                    pe.wait_ge(a3_ready, t * 2 - 2)
                    for pair in range(2):
                        count(pe, msg_ready, t * 2 - 5 + pair)
                        for i2 in range(2):
                            tile = pair * 2 + i2
                            o = wps[pair][:, i2 * HID:(i2 + 1) * HID]
                            nc.tensor.matmul(o, ones_bf[:], b3_parts[:], start=True, stop=False)
                            for kk in range(2):
                                i = nc.tensor.matmul(o, a3[c2][:, kk, tile * P:(tile + 1) * P], f3_sb[:, kk, :],
                                                     start=False, stop=kk == 1)
                        i.then_inc(w_ready, 1)
                if k % 2 == 1:
                    s = n * 2 + (k + 1) // 2
                    if exists(s, N_SUPER):
                        layer1(s, (k + 1) // 2 % 2)

            layer1(0, 0)
            pe.wait_ge(hn_ready, N_GROUPS)
            edge_loop(pe, step, 3)
            pe.wait_ge(sum_ready, 2 * N_CHUNK)

            node_loop(pe, lambda g, n, half: group(g, hg, half, fn_ready, ft_ready, fnT_ready, gp_ready, gz_ready, gw_sb), 0)

        @block.vector
        def _(ve):
            V = nc.vector
            V.memset(half_pi[:], 0.5 * np.pi).then_inc(v_small, 1)
            V.memset(ones_bf[:], 1.0).then_inc(v_small, 1)
            V.memset(b3_parts[:], 0.0).then_inc(v_small, 1)

            ve.wait_ge(dist_in, 16)
            V.tensor_scalar(ev[0][:], dist_c[:], 0.5 / CUTOFF, ROUND, ALU.mult, ALU.add).then_inc(v_env, 1)
            ve.wait_ge(v_env, 1)
            V.tensor_scalar(ev[1][:], ev[0][:], -ROUND, None, ALU.add).then_inc(v_env, 1)
            ve.wait_ge(v_env, 2)
            V.scalar_tensor_tensor(ev[2][:], dist_c[:], 0.5 / CUTOFF, ev[1][:], ALU.mult, ALU.subtract).then_inc(v_env, 1)
            ve.wait_ge(v_env, 3)
            V.scalar_tensor_tensor(ev[0][:], ev[2][:], -1.0, ev[2][:], ALU.mult, ALU.max).then_inc(v_env, 1)
            ve.wait_ge(v_env, 4)
            V.tensor_scalar(ev[2][:], dist_c[:], CUTOFF, 0.5, ALU.is_lt, ALU.mult).then_inc(v_env, 1)
            ve.wait_ge(a_env, 1)
            ve.wait_ge(v_env, 5)
            V.scalar_tensor_tensor(ev[0][:], ev[1][:], 1.0, ev[2][:], ALU.add, ALU.mult).then_inc(env_ok, 1)

            def layernorm(g, half, src, dst, wait, base):
                for t in range(G_T):
                    i = V.bn_stats(st6[:, t, :], src[:, t, :])
                i.then_inc(ln_step, 1)
                ve.wait_ge(ln_step, base + 1)
                ve.sem_inc(ve_pass, 1)
                for t in range(G_T):
                    i = V.bn_aggr(st2[half][:, t, :], st6[:, t, :])
                i.then_inc(ln_step, 1)
                ve.wait_ge(ln_step, base + 2)
                V.tensor_scalar(var_e[:], st2[half][:, :, 1], EPS_LN, None, ALU.add).then_inc(ln_step, 1)
                ve.wait_ge(ln_step, base + 3)
                V.tensor_scalar(seed[:], var_e[:].bitcast(I32), 1, None, ALU.logical_shift_right).then_inc(ln_step, 1)
                ve.wait_ge(ln_step, base + 4)
                V.tensor_scalar(rstd[0][:].bitcast(I32), seed[:], -1.0, float(0x5F3759DF), ALU.mult, ALU.add).then_inc(ln_step, 1)
                for k in range(3):
                    ve.wait_ge(ln_step, base + 5 + 3 * k)
                    V.scalar_tensor_tensor(yy[:], rstd[k][:], -0.5, rstd[k][:], ALU.mult, ALU.mult).then_inc(ln_step, 1)
                    ve.wait_ge(ln_step, base + 6 + 3 * k)
                    V.tensor_tensor(yy[:], yy[:], var_e[:], ALU.mult).then_inc(ln_step, 1)
                    ve.wait_ge(ln_step, base + 7 + 3 * k)
                    V.scalar_tensor_tensor(rstd[k + 1][:], yy[:], 1.5, rstd[k][:], ALU.add, ALU.mult).then_inc(ln_step, 1)
                ve.wait_ge(ln_step, base + LN_STEPS)
                for t in range(G_T):
                    i = V.tensor_scalar(dst[:, t, :], src[:, t, :], st2[half][:, t, 0:1], rstd[3][:, t:t + 1], ALU.subtract, ALU.mult)
                return i

            def nodes(g, n, half):
                if exists(g, N_GROUPS):
                    ve.wait_ge(x_in[half], 16 * (n + 1))
                    count(ve, h_out[half], 16 * n)
                    count(ve, t_ready, g - 1)
                    layernorm(g, half, xg[half], hg[half], None, g * (LN_STEPS + 1)).then_inc(ln_step, 1)
                    ve.wait_ge(ln_step, g * (LN_STEPS + 1) + LN_STEPS + 1)
                    V.tensor_scalar(hg[half][:], hg[half][:], 0.0, None, ALU.max).then_inc(h_ready, 1)
                if exists(g - 1, N_GROUPS):
                    o = og[1 - half]
                    if isinstance(g, int) and g == 1:
                        ve.wait_ge(bc_in, 16 * N_BC)
                    ve.wait_ge(np_ready, g)
                    count(ve, hn_out[1 - half], (n - 1 + half) * 16)
                    for b, bank in enumerate((z3[0], z3[1], wps[0])):
                        w = min(2, G_T - 2 * b)
                        i = V.tensor_tensor(o[:, 2 * b:2 * b + w, :], bank[:, 0:w * HID].rearrange("p (a h) -> p a h", h=HID),
                                            per_tile(nb_bc, w), ALU.add)
                    i.then_inc(hn_ready, 1)

            def small_weights():
                ve.wait_ge(wts_in, 16 * N_WTS)
                V.scalar_tensor_tensor(rw_sb[:], wid_sb[:], -1.0, wid_sb[:], ALU.mult, ALU.max).then_inc(v_small, 1)
                ve.wait_ge(v_small, 4)
                V.tensor_scalar(rw_sb[:], rw_sb[:], EPS_W, None, ALU.add).then_inc(v_small, 1)
                ve.wait_ge(v_small, 5)
                V.reciprocal(rw_sb[:], rw_sb[:]).then_inc(v_small, 1)
                V.tensor_copy(b3_bf[:, 0, :], b3_rows[:, 0, :]).then_inc(b3_step, 1)
                for k in range(2):
                    ve.wait_ge(b3_step, 2 * k + 1)
                    V.tensor_tensor(b3_rows[:, k + 1, :], b3_rows[:, k, :], b3_bf[:, k, :], ALU.subtract).then_inc(b3_step, 1)
                    ve.wait_ge(b3_step, 2 * k + 2)
                    V.tensor_copy(b3_bf[:, k + 1, :], b3_rows[:, k + 1, :]).then_inc(b3_step, 1)
                ve.wait_ge(b3_step, 5)
                for k in range(3):
                    V.tensor_copy(b3_parts[32 * k:32 * k + 1, :], b3_bf[32 * k:32 * k + 1, k, :]).then_inc(b3_step, 1)
                ve.wait_ge(fuse_mm, 1)
                V.tensor_copy(w23_sb[:], z3[0][:, 0:HID]).then_inc(fuse_v, 1)
                V.tensor_tensor(b23_sb[:], z3[1][:, 0:2], fb1_sb[:], ALU.add).then_inc(fuse_v, 1)
                ve.wait_ge(p_step, 3)
                V.tensor_copy(dump_f[:], dump_i[:]).then_inc(v_small, 1)
                ve.wait_ge(p_const, 2)
                ve.wait_ge(v_small, 7)
                ve.wait_ge(b3_step, 8)

            small_weights()
            node_loop(ve, nodes, 1)

            def scaled(s, n, q):
                ve.wait_ge(d_in[q], 64 * (n + 1))
                count(ve, sq_ready, s - 1)
                V.tensor_scalar(u[q][:], d_bc[q][:], cen_sb[:], rw_sb[:], ALU.subtract, ALU.mult).then_inc(u_ready, 1)

            def basis(s, q):
                ve.wait_ge(exp_ready, s + 1)
                count(ve, z1_ready, s - 1)
                V.tensor_tensor(r_in[q][:], rbf[q][:], e_bc[q][:], ALU.mult).then_inc(r_ready, 1)

            def targets(s, n, q):
                ve.wait_ge(idx_in[q], 48 * (n + 1))
                count(ve, c_ready, s * 4 - 4)
                sc = src_c[q][:]
                V.tensor_tensor(same[q][:], src_r[q][:].rearrange("p (j e) -> p j e", j=8),
                                sc.rearrange("p (j a) -> p j a", a=1).to_broadcast([P, 8, P]), ALU.is_equal).then_inc(same_ready, 1)
                V.tensor_scalar(to_dump[:], sc, -1.0, dump_f[:], ALU.mult, ALU.add).then_inc(dump_ready, 1)
                ve.wait_ge(same_ready, s + 1)
                V.tensor_tensor(same_lo[:], same[q][:], lower[:].rearrange("p (a e) -> p a e", a=1).to_broadcast([P, 8, P]),
                                ALU.mult).then_inc(lo_ready, 1)
                ve.wait_ge(lo_ready, s + 1)
                V.tensor_reduce(n_before[:], same_lo[:], AX_X, ALU.add).then_inc(cnt_ready, 1)
                ve.wait_ge(cnt_ready, s + 1)
                ve.wait_ge(dump_ready, s + 1)
                V.scalar_tensor_tensor(is_dup[:], n_before[:], 1.0, to_dump[:], ALU.min, ALU.mult).then_inc(dup_ready, 1)
                ve.wait_ge(dup_ready, s + 1)
                for i in range(N_TAB):
                    count(ve, scat[i], (s - 1) * (16 * 8 // N_TAB))
                V.tensor_tensor(target[q][:], is_dup[:], sc, ALU.add).then_inc(tgt_ready, 1)

            def messages(c, n, k):
                s_half = k % 2
                q = (k % 4) // 2
                n2 = n + (k - k % 4) // 4
                for pair in range(2):
                    ve.wait_ge(w_ready, c * 2 + pair + 1)
                    ve.wait_ge(gath[q][s_half * 2 + pair], 32 * (n2 + 1))
                    count(ve, c_ready, c * 2 - 3 + pair)
                    V.tensor_tensor(msg[s_half][pair][:].rearrange("p a h -> p (a h)"), wps[pair][:],
                                    hn_g[q][s_half * 2 + pair][:].rearrange("p a h -> p (a h)"), ALU.mult).then_inc(msg_ready, 1)

            def step(t, n, k):
                if k == 1 and exists(n * 2 + 2, N_SUPER):
                    for i in range(2):
                        scaled(n * 2 + 2 + i, n + 1, i)
                if k % 2 == 0:
                    s = n * 2 + k // 2 - 1
                    if exists(s, N_SUPER):
                        targets(s, n - 1 + k // 2, (k // 2 + 1) % 2)
                if exists(t - 2):
                    messages(t - 2, n, k - 2)
                if k == 2 and exists(n * 2 + 2, N_SUPER):
                    for i in range(2):
                        basis(n * 2 + 2 + i, i)

            for s in range(2):
                scaled(s, 0, s)
            for s in range(2):
                basis(s, s)
            edge_loop(ve, step, 3)

            def gated(g, n, half):
                for b, bank in enumerate((z3[0], z3[1], wps[0])):
                    w = min(2, G_T - 2 * b)
                    if b == 0:
                        ve.wait_ge(gp_ready, g + 1)
                        count(ve, out_st[half], 16 * n)
                    i = V.tensor_tensor(og[half][:, 2 * b:2 * b + w, :], bank[:, 0:w * HID].rearrange("p (a h) -> p a h", h=HID),
                                        per_tile(gb_bc, w), ALU.add)
                i.then_inc(gz_ready, 1)

            def finished(g, n, half):
                ve.wait_ge(sg_ready, g + 1)
                V.tensor_tensor(tab[half][1][:], hg[half][:], tab[half][0][:], ALU.mult).then_inc(fg_ready, 1)
                ve.wait_ge(fg_ready, g + 1)
                V.tensor_tensor(og[half][:], tab[half][1][:], xg[half][:], ALU.add).then_inc(out_ready, 1)

            LN0 = N_GROUPS * (LN_STEPS + 1)
            F_STEPS = LN_STEPS + 3

            def last(g, n, half):
                if exists(g, N_GROUPS):
                    base = g * F_STEPS + LN0
                    ve.wait_ge(tab_in[half], 16 * (N_TAB + 1) * (n + 1))
                    V.tensor_tensor(tab[half][0][:], tab[half][0][:], tab[half][1][:], ALU.add).then_inc(ln_step, 1)
                    ve.wait_ge(ln_step, base + 1)
                    count(ve, ft_ready, g - 1)
                    layernorm(g, half, tab[half][0], hg[half], None, base + 1).then_inc(ln_step, 1)
                    ve.wait_ge(ln_step, base + LN_STEPS + 2)
                    V.tensor_tensor(hg[half][:], hg[half][:], per_tile(lg_bc), ALU.mult).then_inc(ln_step, 1)
                    ve.wait_ge(ln_step, base + LN_STEPS + 3)
                    V.tensor_tensor(hg[half][:], hg[half][:], per_tile(lb_bc), ALU.add).then_inc(fn_ready, 1)
                if exists(g - 1, N_GROUPS):
                    gated(g - 1, n - 1 + half, 1 - half)
                    finished(g - 1, n - 1 + half, 1 - half)

            node_loop(ve, last, 1)


_INS = ["x", "src_cols", "src_rows", "dst_cols", "dist", "centers", "widths", "w1", "b1", "w2t", "b2", "f1", "fb1",
        "f2", "fb2", "f3", "fb3", "node_w", "node_b", "ln_g", "ln_b", "gate_w", "gate_b"]


def kernel(x, src, dst, edge_weight, L0_gnn_centers, L0_gnn_widths, L0_gnn_rbf_w1, L0_gnn_rbf_b1,
           L0_gnn_rbf_w2, L0_gnn_rbf_b2, L0_gnn_filt_w1, L0_gnn_filt_b1, L0_gnn_filt_w2, L0_gnn_filt_b2,
           L0_gnn_filt_w3, L0_gnn_filt_b3, L0_gnn_node_w, L0_gnn_node_b, L0_gnn_ln_g, L0_gnn_ln_b,
           L0_gnn_gate_w, L0_gnn_gate_b):
    import concourse.bacc as bacc
    from concourse.bass_utils import run_bass_kernel_spmd

    def pad(a, n, value=0):
        a = np.asarray(a)
        return np.concatenate([a, np.full((n - a.shape[0],) + a.shape[1:], value, a.dtype)])

    def columns(a):
        return np.ascontiguousarray(a.reshape(N_SUPER, 8, TILE).transpose(0, 2, 1))

    def halves(a):
        return np.ascontiguousarray(np.asarray(a).reshape(2, P).T)

    src_p = pad(src, E_PAD, N_PAD - 1)
    dst_p = pad(dst, E_PAD, 0)
    w2t = np.asarray(L0_gnn_rbf_w2).T
    arrays = {
        "x": pad(x, N_PAD), "src_cols": columns(src_p), "src_rows": src_p, "dst_cols": columns(dst_p),
        "dist": pad(edge_weight, E_PAD), "centers": L0_gnn_centers,
        "widths": np.concatenate([np.asarray(L0_gnn_widths)] * 2).reshape(P, 1),
        "w1": L0_gnn_rbf_w1, "b1": L0_gnn_rbf_b1, "w2t": np.concatenate([w2t, w2t], axis=1), "b2": L0_gnn_rbf_b2,
        "f1": L0_gnn_filt_w1, "fb1": halves(L0_gnn_filt_b1), "f2": L0_gnn_filt_w2, "fb2": halves(L0_gnn_filt_b2),
        "f3": L0_gnn_filt_w3, "fb3": L0_gnn_filt_b3, "node_w": L0_gnn_node_w, "node_b": L0_gnn_node_b,
        "ln_g": L0_gnn_ln_g, "ln_b": L0_gnn_ln_b, "gate_w": L0_gnn_gate_w, "gate_b": L0_gnn_gate_b,
    }
    arrays = {k: np.ascontiguousarray(v) for k, v in arrays.items()}
    nc = bacc.Bacc("TRN2", target_bir_lowering=False, num_devices=1)
    args = [nc.dram_tensor(n, arrays[n].shape, mybir.dt.from_np(arrays[n].dtype), kind="ExternalInput").ap() for n in _INS]
    args.append(nc.dram_tensor("out", (N_PAD, HID), F32, kind="ExternalOutput").ap())
    build(nc, *args)
    result = run_bass_kernel_spmd(nc, [arrays], core_ids=[0])
    return result.results[0]["out"][:N_NODES]
```

```python
from contextlib import ExitStack

import numpy as np

import concourse.bass as bass
from concourse import mybir

P = 128
HID = 256
R = 64
N_NODES = 6250
N_EDGES = 100000

G_T = 5
G_ROWS = G_T * P
N_GROUPS = 10
SLOTS = 3
N_PAD = N_GROUPS * G_ROWS
DUMP = N_PAD
T_ROWS = N_PAD + P

TILE = P
CHUNK = 4 * TILE
SUPER = 2 * CHUNK
N_SUPER = -(-N_EDGES // SUPER)
N_SUPER += N_SUPER % 2
N_CHUNK = 2 * N_SUPER
E_PAD = N_SUPER * SUPER
E_COLS = E_PAD // P
N_TAB = 2

CUTOFF = 10.0
EPS_W = 1e-05
EPS_LN = 1e-05
ROUND = 1.5 * 2.0 ** 23

F32 = mybir.dt.float32
F32R = mybir.dt.float32r
BF16 = mybir.dt.bfloat16
I32 = mybir.dt.int32
ALU = mybir.AluOpType
ACT = mybir.ActivationFunctionType
AX_X = mybir.AxisListType.X


def build(nc, x, src_cols, src_rows, dst_cols, dist, centers, widths, w1, b1, w2t, b2, f1, fb1,
          f2, fb2, f3, fb3, node_w, node_b, ln_g, ln_b, gate_w, gate_b, out):
    with ExitStack() as ctx:
        def sb(name, shape, dt=F32):
            return ctx.enter_context(nc.sbuf_tensor(name, shape, dt))

        def ps(name):
            return ctx.enter_context(nc.psum_tensor(name, [P, 512], F32))

        def sem(name):
            return ctx.enter_context(nc.semaphore(name))

        hn_tab = nc.dram_tensor("hn_tab", [N_PAD, HID], F32).ap()
        agg = [nc.dram_tensor(f"agg{i}", [T_ROWS, HID], F32).ap() for i in range(N_TAB)]
        env_d = nc.dram_tensor("env_d", [E_PAD], F32).ap()

        w1_sb = sb("w1_sb", [P, P])
        w2t_sb = sb("w2t_sb", [R, P])
        f1_sb = sb("f1_sb", [R, HID])
        w23_sb = sb("w23_sb", [P, HID])
        w23_p = [sb(f"w23_p{i}", [P, HID], F32R) for i in range(2)]
        f2_p = [sb(f"f2_p{i}", [P, 2, HID], F32R) for i in range(2)]
        f3_p = [sb(f"f3_p{i}", [P, 2, HID], F32R) for i in range(2)]
        nw_sb = sb("nw_sb", [P, 2, HID])
        gw_sb = sb("gw_sb", [P, 2, HID])
        b1_sb = sb("b1_sb", [P, 1])
        b2_sb = sb("b2_sb", [R, 1])
        fb1_sb = sb("fb1_sb", [P, 2])
        b23_sb = sb("b23_sb", [P, 2])
        fb2_sb = sb("fb2_sb", [P, 2])
        bias_bf = sb("bias_bf", [96, 3, 3, HID], BF16)
        bias_parts = sb("bias_parts", [96, 3, HID], BF16)
        ones_bf = sb("ones_bf", [96, P], BF16)
        lg_bc = sb("lg_bc", [P, HID])
        lb_bc = sb("lb_bc", [P, HID])
        cen_sb = sb("cen_sb", [P, 1])
        wid_sb = sb("wid_sb", [P, 1])
        rw_sb = sb("rw_sb", [P, 1])
        neg_cen = sb("neg_cen", [P, 1])
        exp_scale = sb("exp_scale", [P, 1])
        ident = sb("ident", [P, P])
        upto = sb("upto", [P, P])
        dump_i = sb("dump_i", [P, 1], I32)
        dump_f = sb("dump_f", [P, 1])
        half_pi = sb("half_pi", [P, 1])
        stage = sb("stage", [P, 4 * E_COLS])
        dist_c = stage[:, 0:E_COLS]
        ev = [stage[:, (i + 1) * E_COLS:(i + 2) * E_COLS] for i in range(3)]
        a1 = stage[:, 0:CHUNK]
        a2 = [stage[:, (1 + m) * CHUNK:(2 + m) * CHUNK] for m in range(2)]
        a3 = [stage[:, (3 + m) * CHUNK:(4 + m) * CHUNK] for m in range(2)]

        N_ROWS = 16 * 2 * HID
        work = sb("work", [P, N_ROWS + 10 * CHUNK])
        rows = work[:, 0:N_ROWS].rearrange("p (a n) -> p a n", a=16)
        hn_g = [[rows[:, 4 * i + j, :] for j in range(4)] for i in range(2)]
        summed = [[rows[:, 8 + 4 * i + j, :] for j in range(4)] for i in range(2)]
        tail = [work[:, N_ROWS + i * CHUNK:N_ROWS + (i + 1) * CHUNK] for i in range(10)]
        d_bc = tail[0:2]
        e_bc = tail[2:4]
        u = tail[4:6]
        r_in = tail[6:8]
        msg = tail[8:10]
        f2_sb, f3_sb = [msg[i].rearrange("p (k n) -> p k n", k=2) for i in range(2)]

        G_LEN = G_T * HID
        own = sb("own", [P, 2 * SLOTS * G_LEN])

        def groups(t, first, n=SLOTS, at=0):
            return [t[:, at + i * G_LEN:at + (i + 1) * G_LEN].rearrange("p (t h) -> p t h", t=G_T) for i in range(first, first + n)]

        xg = groups(work, 0, at=N_ROWS)
        hT = groups(work, 0)
        og = groups(work, SLOTS)
        hg = groups(own, 0)
        zeros = groups(own, SLOTS, 1)[0]
        bias_rows = own[0:96, 4 * G_LEN:4 * G_LEN + 9 * HID].rearrange("p (k b n) -> p k b n", k=3, b=3)
        f_t0 = groups(work, 0)
        f_t1 = groups(work, SLOTS)
        f_n = groups(own, 0)
        f_x = groups(own, SLOTS)
        f_o = groups(work, 2 * SLOTS)
        f_T = groups(work, 3 * SLOTS, 1) + groups(stage, 0, 2)
        st6 = sb("st6", [P, G_T, 6])
        st2 = [sb(f"st2{i}", [P, G_T, 2]) for i in range(SLOTS)]
        var_e = sb("var_e", [P, G_T])
        seed = sb("seed", [P, G_T], I32)
        yy = sb("yy", [P, G_T])
        newton = [sb(f"newton{i}", [P, G_T]) for i in range(3)]
        rstd = [sb(f"rstd{i}", [P, G_T]) for i in range(SLOTS)]
        shift = [sb(f"shift{i}", [P, G_T]) for i in range(SLOTS)]

        src_r = [sb(f"src_r{i}", [P, SUPER], I32) for i in range(2)]
        src_c = [sb(f"src_c{i}", [P, 8], I32) for i in range(2)]
        dst_c = [sb(f"dst_c{i}", [P, 8], I32) for i in range(2)]
        a1_p = [[sb(f"a1_p{i}{j}", [P, CHUNK], F32R) for j in range(2)] for i in range(2)]
        same = [sb(f"same{i}", [P, 8, P], F32R) for i in range(2)]
        n_upto = sb("n_upto", [P, 8])
        is_dup = sb("is_dup", [P, 8])
        to_dump = sb("to_dump", [P, 8])
        src_f = sb("src_f", [P, 8])
        target = [sb(f"target{i}", [P, 8], I32) for i in range(2)]
        a2_p = [[sb(f"a2_p{i}{j}", [P, 2, CHUNK], F32R) for j in range(2)] for i in range(2)]
        a3_p = [[sb(f"a3_p{i}{j}", [P, 2, CHUNK], F32R) for j in range(2)] for i in range(2)]
        msg_p = [[[sb(f"msg_p{i}{j}{k}", [P, 2 * HID], F32R) for k in range(2)] for j in range(2)] for i in range(2)]

        z1 = ps("z1")
        z2 = [ps("z2a"), ps("z2b")]
        z3 = [ps("z3a"), ps("z3b")]
        wps = [ps("wa"), ps("wb")]
        cps = [ps("cps"), z1]

        w1_clear = sem("w1_clear")
        wts_in = sem("wts_in")
        bc_in = sem("bc_in")
        dist_in = sem("dist_in")
        p_step = sem("p_step")
        pool_pass = sem("pool_pass")
        ve_pass = sem("ve_pass")
        p_const = sem("p_const")
        x_in = [sem(f"x_in{i}") for i in range(SLOTS)]
        hn_free = [sem(f"hn_free{i}") for i in range(SLOTS)]
        h_out = [sem(f"h_out{i}") for i in range(SLOTS)]
        zeroed = sem("zeroed")
        v_env = sem("v_env")
        a_env = sem("a_env")
        env_ok = sem("env_ok")
        env_out = sem("env_out")
        fuse_mm = sem("fuse_mm")
        fuse_v = sem("fuse_v")
        bias_step = sem("bias_step")
        bias_in = sem("bias_in")
        v_small = sem("v_small")
        ln_step = sem("ln_step")
        nrm_ready = sem("nrm_ready")
        h_ready = sem("h_ready")
        t_ready = sem("t_ready")
        hT_ready = sem("hT_ready")
        np_ready = sem("np_ready")
        hn_ready = sem("hn_ready")
        tab_in = [sem(f"tab_in{i}") for i in range(SLOTS)]
        fx_in = [sem(f"fx_in{i}") for i in range(SLOTS)]
        fs_ready = sem("fs_ready")
        fc_ready = sem("fc_ready")
        fn_ready = sem("fn_ready")
        ft_ready = sem("ft_ready")
        fnT_ready = sem("fnT_ready")
        gp_ready = sem("gp_ready")
        sg_ready = sem("sg_ready")
        fg_ready = sem("fg_ready")
        out_ready = sem("out_ready")
        out_free = [sem(f"out_free{i}") for i in range(SLOTS)]

        d_in = [sem("d_in0"), sem("d_in1")]
        dst_in = [sem("dst_in0"), sem("dst_in1")]
        src_in = [sem("src_in0"), sem("src_in1")]
        gath = [[sem(f"gath{i}_{j}") for j in range(4)] for i in range(2)]
        scat = [sem(f"scat{i}") for i in range(N_TAB)]
        sq_ready = sem("sq_ready")
        exp_ready = sem("exp_ready")
        r_ready = sem("r_ready")
        z1_ready = sem("z1_ready")
        a1_ready = sem("a1_ready")
        z2_ready = sem("z2_ready")
        a2_ready = sem("a2_ready")
        z3_ready = sem("z3_ready")
        a3_ready = sem("a3_ready")
        lo1_ready = sem("lo1_ready")
        lo2_ready = sem("lo2_ready")
        lo3_ready = sem("lo3_ready")
        part_ready = sem("part_ready")
        w_ready = sem("w_ready")
        msg_ready = sem("msg_ready")
        mhi_ready = sem("mhi_ready")
        mlo_ready = sem("mlo_ready")
        cnt_ready = sem("cnt_ready")
        dup_ready = sem("dup_ready")
        dump_ready = sem("dump_ready")
        tgt_ready = sem("tgt_ready")
        c_ready = sem("c_ready")
        sum_ready = sem("sum_ready")

        N_WTS = 15
        N_BC = 2
        SLOT_USES = [len(range(i, N_GROUPS, SLOTS)) for i in range(SLOTS)]
        LN_STEPS = 14
        x_v = x.rearrange("(g p t) h -> g p t h", p=P, t=G_T)
        out_v = out.rearrange("(g p t) h -> g p t h", p=P, t=G_T)
        hn_v = hn_tab.rearrange("(g p t) h -> g p t h", p=P, t=G_T)
        agg_v = [a[0:N_PAD, :].rearrange("(g p t) h -> g p t h", p=P, t=G_T) for a in agg]
        dist_ch = dist.rearrange("(c a e) -> c a e", a=1, e=CHUNK)
        env_ch = env_d.rearrange("(c a e) -> c a e", a=1, e=CHUNK)
        srow_v = src_rows.rearrange("(s a e) -> s a e", a=1, e=SUPER)

        def row(v, n=P):
            return v.rearrange("(a n) -> a n", a=1).to_broadcast([n, v.shape[0]])

        def col(v):
            return v.rearrange("(n a) -> n a", a=1)

        def count(engine, semaphore, n):
            if not isinstance(n, int) or n > 0:
                engine.wait_ge(semaphore, n)

        def node_loop(eng, step, extra):
            for g in range(SLOTS):
                step(g, g // SLOTS, g % SLOTS)
            with eng.Fori(1, N_GROUPS // SLOTS) as it:
                for slot in range(SLOTS):
                    step(it * SLOTS + slot, it, slot)
            for g in range(N_GROUPS // SLOTS * SLOTS, N_GROUPS + extra):
                step(g, g // SLOTS, g % SLOTS)

        def before(n, slot, d):
            return n + (slot - d) // SLOTS, (slot - d) % SLOTS

        def edge_loop(eng, step, extra):
            for t in range(8):
                step(t, t // 4, t % 4)
            with eng.Fori(2, N_CHUNK // 4 - 1) as it:
                for k in range(4):
                    step(it * 4 + k, it, k)
            for t in range(N_CHUNK - 4, N_CHUNK + extra):
                step(t, t // 4, t % 4)

        TERMS = ((0, 0), (0, 1), (1, 0))

        def exists(c, last=N_CHUNK):
            return not isinstance(c, int) or 0 <= c < last

        block = ctx.enter_context(nc.Block())

        @block.sync
        def _(sp):
            def dst_of(s, n, q):
                for j in range(4):
                    count(sp, gath[q][j], 32 * n)
                sp.dma_start(dst_c[q][:], dst_cols[s]).then_inc(dst_in[q], 16)

            def src_of(s, q):
                count(sp, tgt_ready, s - 1)
                sp.dma_start(src_r[q][:], srow_v[s].to_broadcast([P, SUPER])).then_inc(src_in[q], 16)
                sp.dma_start(src_c[q][:], src_cols[s]).then_inc(src_in[q], 16)

            def nodes(g, n, slot):
                if exists(g, N_GROUPS):
                    count(sp, h_ready, g - 2)
                    sp.dma_start(xg[slot], x_v[g]).then_inc(x_in[slot], 16)
                if isinstance(g, int) and g == 0:
                    sp.dma_start(dist_c, dist.rearrange("(p c) -> p c", p=P)).then_inc(dist_in, 16)
                if isinstance(g, int) and g == N_GROUPS - 1:
                    for q in range(2):
                        dst_of(q, 0, q)
                        src_of(q, q)
                    sp.wait_ge(env_ok, 1)
                    sp.dma_start(env_d.rearrange("(p c) -> p c", p=P), ev[0]).then_inc(env_out, 16)
                if exists(g - 1, N_GROUPS):
                    sp.wait_ge(h_ready, g)
                    sp.dma_start(agg_v[0][g - 1], hg[(slot - 1) % SLOTS]).then_inc(h_out[(slot - 1) % SLOTS], 16)

            node_loop(sp, nodes, 1)

            sp.wait_ge(env_out, 16)

            def distances(s, q):
                count(sp, r_ready, s - 1)
                for half in range(2):
                    part = slice(half * R, half * R + R)
                    sp.dma_start(d_bc[q][part, :], dist_ch[s * 2 + half].to_broadcast([R, CHUNK])).then_inc(d_in[q], 16)
                    sp.dma_start(e_bc[q][part, :], env_ch[s * 2 + half].to_broadcast([R, CHUNK])).then_inc(d_in[q], 16)

            def two(n, more=True):
                dst_of(n * 2, n, 0)
                if more:
                    for q in range(2):
                        distances(n * 2 + 2 + q, q)
                src_of(n * 2, 0)
                dst_of(n * 2 + 1, n, 1)
                src_of(n * 2 + 1, 1)

            for s in range(4):
                distances(s, s % 2)
            with sp.Fori(1, N_SUPER // 2 - 1) as it:
                two(it)
            two(N_SUPER // 2 - 1, more=False)

            for i in range(N_TAB):
                sp.wait_ge(scat[i], 16 * N_SUPER * 8 // N_TAB)

            sp.wait_ge(sum_ready, 2 * N_CHUNK)

            def last(g, n, slot):
                count(sp, fn_ready, g - 2)
                for i, t in enumerate((f_t0, f_t1)):
                    sp.dma_start(t[slot], agg_v[i][g]).then_inc(tab_in[slot], 16)

            node_loop(sp, last, 0)
            for i in range(SLOTS):
                sp.wait_ge(out_free[i], 16 * (SLOT_USES[i] + 1))

        @block.gpsimd
        def _(pool):
            pool.memset(w1_sb[:], 0.0).then_inc(w1_clear, 1)
            pool.memset(ident[:], 0.0).then_inc(p_step, 1)
            pool.memset(upto[:], 1.0).then_inc(p_step, 1)
            pool.iota(dump_i[:], pattern=[[0, 1]], base=DUMP, channel_multiplier=1).then_inc(p_step, 1)
            pool.memset(zeros, 0.0).then_inc(p_step, 1)
            pool.wait_ge(p_step, 4)
            pool.affine_select(out=ident[:], in_=ident[:], compare_op=ALU.not_equal, fill=1.0,
                               base=0, pattern=[[-1, P]], channel_multiplier=1).then_inc(p_const, 1)
            pool.affine_select(out=upto[:], in_=upto[:], compare_op=ALU.is_ge, fill=0.0,
                               base=0, pattern=[[-1, P]], channel_multiplier=1).then_inc(p_const, 1)
            n_zero = 0
            for i in range(N_TAB):
                pool.dma_start(agg[i][DUMP:T_ROWS, :], zeros[:, 0, :]).then_inc(zeroed, 16)
                n_zero += 1
            for i in range(1, N_TAB):
                for g in range(N_GROUPS):
                    pool.wait_ge(h_ready, g + 1)
                    pool.dma_start(agg_v[i][g], zeros).then_inc(zeroed, 16)
                    n_zero += 1

            for i in range(SLOTS):
                pool.wait_ge(hn_free[i], 16 * (SLOT_USES[i] + 1))

            pool.wait_ge(zeroed, 16 * n_zero)

            def gather(s, n, q, j):
                pool.indirect_dma_start(
                    out=hn_g[q][j // 2][:, (j % 2) * HID:(j % 2 + 1) * HID], out_offset=None, in_=hn_tab,
                    in_offset=bass.IndirectOffsetOnAxis(ap=dst_c[q][:, j:j + 1], axis=0),
                ).then_inc(gath[q][j // 2], 16)

            def scatter(s, n, q, j):
                i = j % N_TAB
                per = 8 // N_TAB
                if j % 2 == 0:
                    pool.wait_ge(sum_ready, s * 4 + j // 2 + 1)
                if j == 0:
                    pool.wait_ge(tgt_ready, s + 1)
                count(pool, scat[i], (s * per + j // N_TAB) * 16)
                if not isinstance(s, int):
                    pool.sem_inc(pool_pass, 1)
                pool.indirect_dma_start(
                    out=agg[i], out_offset=bass.IndirectOffsetOnAxis(ap=target[q][:, j:j + 1], axis=0),
                    in_=summed[q][j // 2][:, (j % 2) * HID:(j % 2 + 1) * HID], in_offset=None, compute_op=ALU.add,
                ).then_inc(scat[i], 16)

            def superchunk(s, n, q):
                if exists(s, N_SUPER):
                    pool.wait_ge(dst_in[q], 16 * (n + 1))
                if isinstance(s, int) and s == 2:
                    for i in range(SLOTS):
                        pool.wait_ge(h_out[i], 16 * SLOT_USES[i])
                for j in range(8):
                    if exists(s, N_SUPER):
                        if j % 2 == 0:
                            count(pool, msg_ready, s * 4 - 8 + j // 2 + 1)
                            if not isinstance(s, int):
                                pool.sem_inc(pool_pass, 1)
                        gather(s, n, q, j)
                    if exists(s - 2, N_SUPER):
                        scatter(s - 2, n - 1, q, j)

            for s in range(4):
                superchunk(s, s // 2, s % 2)
            with pool.Fori(2, N_SUPER // 2) as it:
                for q in range(2):
                    superchunk(it * 2 + q, it, q)
            for s in range(N_SUPER, N_SUPER + 2):
                superchunk(s, s // 2, s % 2)

            def last(g, n, slot):
                if exists(g, N_GROUPS):
                    pool.wait_ge(tab_in[slot], 32 * (n + 1))
                    pool.tensor_tensor(f_t0[slot], f_t0[slot], f_t1[slot], ALU.add).then_inc(fs_ready, 1)
                if exists(g - 3, N_GROUPS):
                    n3, slot3 = before(n, slot, 3)
                    pool.wait_ge(sg_ready, g - 2)
                    pool.tensor_tensor(f_o[slot3], f_o[slot3], f_n[slot3], ALU.mult).then_inc(fg_ready, 1)
                    pool.wait_ge(fx_in[slot3], 16 * (n3 + 1))
                    pool.wait_ge(fg_ready, g - 2)
                    pool.tensor_tensor(f_o[slot3], f_o[slot3], f_x[slot3], ALU.add).then_inc(out_ready, 1)

            node_loop(pool, last, 3)

        @block.scalar
        def _(act):
            def transposed(g, T, ready, used, done):
                act.wait_ge(ready, g + 1)
                count(act, used, g - 2)
                flat = T.rearrange("p t h -> p (t h)")
                for b, bank in enumerate((z1, z2[0], z2[1])):
                    n = min(512, G_LEN - 512 * b)
                    i = act.activation(flat[:, 512 * b:512 * b + n], bank[:, 0:n], ACT.Copy)
                i.then_inc(done, 1)

            def weights():
                for k, v in enumerate((fb3, node_b, gate_b)):
                    act.dma_start(bias_rows[:, 0, k, :], row(v, 96)).then_inc(bias_in, 16)
                act.dma_start(nw_sb[:], node_w.rearrange("(k p) n -> p k n", p=P)).then_inc(bias_in, 16)
                act.wait_ge(w1_clear, 1)
                for dst, src in ((w1_sb[0:R, 0:R], w1), (w1_sb[R:P, R:P], w1),
                                 (w2t_sb[:], w2t), (f1_sb[:], f1),
                                 (f2_sb, f2.rearrange("(k p) n -> p k n", p=P)),
                                 (f3_sb, f3.rearrange("(k p) n -> p k n", p=P)),
                                 (gw_sb[:], gate_w.rearrange("(k p) n -> p k n", p=P)),
                                 (b1_sb[0:R, :], col(b1)), (b1_sb[R:P, :], col(b1)),
                                 (b2_sb[:], col(b2)),
                                 (fb1_sb[:], fb1), (fb2_sb[:], fb2),
                                 (cen_sb[0:R, :], col(centers)), (cen_sb[R:P, :], col(centers)),
                                 (wid_sb[:], widths)):
                    act.dma_start(dst, src).then_inc(wts_in, 16)
                for dst, src in ((lg_bc[:], ln_g), (lb_bc[:], ln_b)):
                    act.dma_start(dst, row(src)).then_inc(bc_in, 16)

            def nodes(g, n, slot):
                if isinstance(g, int) and g == 1:
                    act.wait_ge(v_small, 1)
                    act.wait_ge(v_env, 4)
                    act.activation(ev[1], ev[0], ACT.Sin, bias=half_pi[:], scale=-2.0 * np.pi).then_inc(a_env, 1)
                if exists(g, N_GROUPS):
                    act.wait_ge(nrm_ready, g + 1)
                    count(act, t_ready, g - 2)
                    count(act, h_out[slot], 16 * n)
                    for t in range(G_T):
                        i = act.activation(hg[slot][:, t, :], xg[slot][:, t, :], ACT.Relu,
                                           bias=shift[slot][:, t:t + 1], scale=rstd[slot][:, t:t + 1])
                    i.then_inc(h_ready, 1)
                if exists(g - 2, N_GROUPS):
                    n2, slot2 = before(n, slot, 2)
                    flat = og[slot2].rearrange("p t h -> p (t h)")
                    act.wait_ge(np_ready, g - 1)
                    act.wait_ge(hn_free[slot2], 16 * (n2 + 1))
                    for b, bank in enumerate((z3[0], z3[1], wps[0])):
                        w = min(512, G_LEN - 512 * b)
                        i = act.activation(flat[:, 512 * b:512 * b + w], bank[:, 0:w], ACT.Copy)
                    i.then_inc(hn_ready, 1)
                    act.wait_ge(hn_ready, g - 1)
                    act.dma_start(hn_v[g - 2], og[slot2]).then_inc(hn_free[slot2], 16)
                if exists(g, N_GROUPS):
                    transposed(g, hT[slot], t_ready, np_ready, hT_ready)

            weights()
            for free in hn_free + out_free:
                act.sem_inc(free, 16)
            node_loop(act, nodes, 2)

            def exps(s0, n):
                for q in range(2):
                    act.wait_ge(d_in[q], 64 * (n + 1))
                    count(act, r_ready, s0 + q - 1)
                    act.activation(u[q], d_bc[q], ACT.Square, bias=neg_cen[:]).then_inc(sq_ready, 1)
                for q in range(2):
                    act.wait_ge(sq_ready, s0 + q + 1)
                    act.activation(u[q], u[q], ACT.Exp, scale=exp_scale[:]).then_inc(exp_ready, 1)

            def silu1(s, q):
                act.wait_ge(z1_ready, s + 1)
                count(act, z2_ready, s * 4 - 4)
                count(act, lo1_ready, s)
                act.activation(a1, z1[:], ACT.Silu, bias=b1_sb[:])
                act.activation(a1_p[q][0][:], z1[:], ACT.Silu, bias=b1_sb[:]).then_inc(a1_ready, 1)

            def step(t, n, k):
                if exists(t):
                    for m in range(2):
                        act.wait_ge(z2_ready, t * 2 + m + 1)
                        if m == 0:
                            count(act, z3_ready, t * 2 - 2)
                        count(act, lo2_ready, t * 2 - 1 + m)
                        act.activation(a2[m], z2[m][:], ACT.Silu, bias=b23_sb[:, m:m + 1])
                        act.activation(a2_p[k % 2][0][:, m, :], z2[m][:], ACT.Silu, bias=b23_sb[:, m:m + 1]).then_inc(a2_ready, 1)
                if k % 2 == 1:
                    s = n * 2 + (k + 1) // 2
                    if exists(s, N_SUPER):
                        silu1(s, (k + 1) // 2 % 2)
                c = t - 3
                q = ((k + 1) // 2) % 2

                def take_sums(pair):
                    if exists(c):
                        act.wait_ge(c_ready, c * 2 + pair + 1)
                        h = (k + 1) % 2
                        slot = 2 * h + pair
                        for i in range(N_TAB):
                            count(act, scat[i], (c * 2 + pair - 7) * (32 // N_TAB))
                        act.activation(summed[q][slot], cps[pair][:], ACT.Copy).then_inc(sum_ready, 1)

                if exists(t - 1):
                    for m in range(2):
                        act.wait_ge(z3_ready, (t - 1) * 2 + m + 1)
                        if m == 0:
                            count(act, w_ready, t * 2 - 4)
                        count(act, lo3_ready, t * 2 - 3 + m)
                        act.activation(a3[m], z3[m][:], ACT.Silu, bias=fb2_sb[:, m:m + 1])
                        act.activation(a3_p[(k + 1) % 2][0][:, m, :], z3[m][:], ACT.Silu, bias=fb2_sb[:, m:m + 1]).then_inc(a3_ready, 1)
                if k == 1 and exists(n * 2 + 2, N_SUPER):
                    exps(n * 2 + 2, n + 1)
                for pair in range(2):
                    take_sums(pair)

            act.wait_ge(v_small, 9)
            exps(0, 0)
            silu1(0, 0)
            edge_loop(act, step, 3)

            def last(g, n, slot):
                if exists(g - 2, N_GROUPS):
                    n2, slot2 = before(n, slot, 2)
                    flat = f_o[slot2].rearrange("p t h -> p (t h)")
                    act.wait_ge(gp_ready, g - 1)
                    act.wait_ge(out_free[slot2], 16 * (n2 + 1))
                    for b, bank in enumerate((z3[0], z3[1], wps[0])):
                        w = min(512, G_LEN - 512 * b)
                        i = act.activation(flat[:, 512 * b:512 * b + w], bank[:, 0:w], ACT.Sigmoid)
                    i.then_inc(sg_ready, 1)
                if exists(g, N_GROUPS):
                    transposed(g, f_T[slot], ft_ready, gp_ready, fnT_ready)
                if exists(g - 3, N_GROUPS):
                    slot3 = before(n, slot, 3)[1]
                    act.wait_ge(out_ready, g - 2)
                    act.dma_start(out_v[g - 3], f_o[slot3]).then_inc(out_free[slot3], 16)
                if exists(g, N_GROUPS):
                    act.dma_start(f_x[slot], x_v[g]).then_inc(fx_in[slot], 16)

            node_loop(act, last, 3)

        @block.tensor
        def _(pe):
            def fuse():
                pe.wait_ge(wts_in, 16 * N_WTS)
                nc.tensor.matmul(wps[1][:, 0:HID], w2t_sb[:], f1_sb[:], start=True, stop=True)
                for m in range(2):
                    i = nc.tensor.matmul(wps[1][:, HID + m:HID + m + 1], f1_sb[:, m * P:(m + 1) * P], b2_sb[:], start=True, stop=True)
                i.then_inc(fuse_mm, 1)

            pe.wait_ge(p_const, 2)

            def group(g, slot, rows_g, T, ready, tr, trT, prod, prod_used, w, bias):
                if exists(g, N_GROUPS):
                    pe.wait_ge(ready, g + 1)
                    count(pe, trT, g)
                    for x_ in range(2 * G_T):
                        bank = (z1, z2[0], z2[1])[x_ // 4]
                        i = nc.tensor.transpose(bank[:, (x_ % 4) * P:(x_ % 4 + 1) * P],
                                                rows_g[slot][:, x_ // 2, (x_ % 2) * P:(x_ % 2 + 1) * P], ident[:])
                    i.then_inc(tr, 1)
                if exists(g - 1, N_GROUPS):
                    pe.wait_ge(trT, g)
                    count(pe, prod_used, g - 1)
                    T_g = T[(slot - 1) % SLOTS]
                    for t in range(G_T):
                        o = (z3[0], z3[1], wps[0])[t // 2][:, (t % 2) * HID:(t % 2 + 1) * HID]
                        nc.tensor.matmul(o, ones_bf[:], bias_parts[:, bias, :], start=True, stop=False)
                        for kk in range(2):
                            i = nc.tensor.matmul(o, T_g[:, t, kk * P:(kk + 1) * P], w[:, kk, :], start=False, stop=kk == 1)
                    i.then_inc(prod, 1)

            def nodes(g, n, slot):
                if isinstance(g, int) and g == 1:
                    pe.wait_ge(bias_in, 64)
                    pe.wait_ge(bias_step, 8)
                group(g, slot, hg, hT, h_ready, t_ready, hT_ready, np_ready, hn_ready, nw_sb, 1)
                if isinstance(g, int) and g == N_GROUPS - 1:
                    fuse()

            node_loop(pe, nodes, 1)

            def layer1(s, q):
                pe.wait_ge(r_ready, s + 1)
                if isinstance(s, int) and s == 0:
                    pe.wait_ge(hT_ready, N_GROUPS)
                count(pe, sum_ready, s * 4 - 8)
                nc.tensor.matmul(z1[:], w1_sb[:], r_in[q][:], start=True, stop=True).then_inc(z1_ready, 1)

            def step(t, n, k):
                if exists(t):
                    h = k % 2
                    part = slice(h * R, h * R + R)
                    q = k // 2
                    if h == 0:
                        pe.wait_ge(a1_ready, n * 2 + q + 1)
                        pe.wait_ge(lo1_ready, n * 2 + q + 1)
                    for m in range(2):
                        count(pe, a2_ready, t * 2 - 1 + m)
                        for x_, (wi, ai) in enumerate(TERMS):
                            i = nc.tensor.matmul(z2[m][:], w23_p[wi][part, m * P:(m + 1) * P], a1_p[q][ai][part, :],
                                                 start=x_ == 0, stop=x_ == 2)
                        i.then_inc(z2_ready, 1)
                if k % 2 == 1:
                    s = n * 2 + (k + 1) // 2
                    if exists(s, N_SUPER):
                        layer1(s, (k + 1) // 2 % 2)
                c = t - 3
                q3 = ((k + 1) // 2) % 2
                h3 = (k + 1) % 2

                def add_equal(pair):
                    if not exists(c):
                        return
                    pe.wait_ge(mlo_ready, c * 2 + pair + 1)
                    if pair == 0 and h3 == 0:
                        pe.wait_ge(cnt_ready, n * 2 + (k + 1) // 2 - 1)
                    count(pe, sum_ready, c * 2 - 1 + pair)
                    if pair == 1 and k % 2 == 1 and exists(n * 2 + (k + 1) // 2, N_SUPER):
                        pe.wait_ge(a1_ready, n * 2 + (k + 1) // 2 + 1)
                    for i2 in range(2):
                        part = slice(i2 * HID, (i2 + 1) * HID)
                        for x_ in range(2):
                            i = nc.tensor.matmul(cps[pair][:, part], same[q3][:, h3 * 4 + pair * 2 + i2, :],
                                                 msg_p[h3][pair][x_][:, part], start=x_ == 0, stop=x_ == 1)
                    i.then_inc(c_ready, 1)

                if exists(t - 1):
                    c1 = (k + 1) % 2
                    pe.wait_ge(a2_ready, t * 2)
                    pe.wait_ge(lo2_ready, t * 2)
                    for m in range(2):
                        count(pe, a3_ready, t * 2 - 3 + m)
                        for kk in range(2):
                            for x_, (wi, ai) in enumerate(TERMS):
                                i = nc.tensor.matmul(z3[m][:], f2_p[wi][:, kk, m * P:(m + 1) * P], a2_p[c1][ai][:, kk, :],
                                                     start=kk + x_ == 0, stop=kk + x_ == 3)
                        i.then_inc(z3_ready, 1)
                c2 = k % 2
                for pair in range(2):
                    add_equal(pair)
                    if exists(t - 2):
                        if pair == 0:
                            pe.wait_ge(a3_ready, t * 2 - 2)
                            pe.wait_ge(lo3_ready, t * 2 - 2)
                        count(pe, msg_ready, t * 2 - 5 + pair)
                        for i2 in range(2):
                            tile = pair * 2 + i2
                            o = wps[pair][:, i2 * HID:(i2 + 1) * HID]
                            nc.tensor.matmul(o, ones_bf[:], bias_parts[:, 0, :], start=True, stop=False)
                            for kk in range(2):
                                for x_, (ai, wi) in enumerate(TERMS):
                                    i = nc.tensor.matmul(o, a3_p[c2][ai][:, kk, tile * P:(tile + 1) * P], f3_p[wi][:, kk, :],
                                                         start=False, stop=kk + x_ == 3)
                        i.then_inc(w_ready, 1)

            layer1(0, 0)
            pe.wait_ge(hn_ready, N_GROUPS)
            pe.wait_ge(part_ready, 6)
            edge_loop(pe, step, 3)
            pe.wait_ge(sum_ready, 2 * N_CHUNK)

            node_loop(pe, lambda g, n, slot: group(g, slot, f_n, f_T, fn_ready, ft_ready, fnT_ready, gp_ready, sg_ready, gw_sb, 2), 1)

        @block.vector
        def _(ve):
            V = nc.vector
            V.memset(half_pi[:], 0.5 * np.pi).then_inc(v_small, 1)
            V.memset(ones_bf[:], 1.0).then_inc(v_small, 1)
            V.memset(bias_parts[:], 0.0).then_inc(v_small, 1)

            def phase():
                ve.wait_ge(dist_in, 16)
                V.tensor_scalar(ev[0], dist_c, 0.5 / CUTOFF, ROUND, ALU.mult, ALU.add).then_inc(v_env, 1)
                ve.wait_ge(v_env, 1)
                V.tensor_scalar(ev[1], ev[0], -ROUND, None, ALU.add).then_inc(v_env, 1)
                ve.wait_ge(v_env, 2)
                V.scalar_tensor_tensor(ev[2], dist_c, 0.5 / CUTOFF, ev[1], ALU.mult, ALU.subtract).then_inc(v_env, 1)
                ve.wait_ge(v_env, 3)
                V.scalar_tensor_tensor(ev[0], ev[2], -1.0, ev[2], ALU.mult, ALU.max).then_inc(v_env, 1)
                ve.wait_ge(v_env, 4)
                V.tensor_scalar(ev[2], dist_c, CUTOFF, 0.5, ALU.is_lt, ALU.mult).then_inc(v_env, 1)

            def envelope():
                ve.wait_ge(a_env, 1)
                ve.wait_ge(v_env, 5)
                V.scalar_tensor_tensor(ev[0], ev[1], 1.0, ev[2], ALU.add, ALU.mult).then_inc(env_ok, 1)

            def layernorm(slot, src, base):
                for t in range(G_T):
                    i = V.bn_stats(st6[:, t, :], src[:, t, :])
                i.then_inc(ln_step, 1)
                ve.wait_ge(ln_step, base + 1)
                ve.sem_inc(ve_pass, 1)
                for t in range(G_T):
                    i = V.bn_aggr(st2[slot][:, t, :], st6[:, t, :])
                i.then_inc(ln_step, 1)
                ve.wait_ge(ln_step, base + 2)
                V.tensor_scalar(var_e[:], st2[slot][:, :, 1], EPS_LN, None, ALU.add).then_inc(ln_step, 1)
                ve.wait_ge(ln_step, base + 3)
                V.tensor_scalar(seed[:], var_e[:].bitcast(I32), 1, None, ALU.logical_shift_right).then_inc(ln_step, 1)
                ve.wait_ge(ln_step, base + 4)
                V.tensor_scalar(newton[0][:].bitcast(I32), seed[:], -1.0, float(0x5F3759DF), ALU.mult, ALU.add).then_inc(ln_step, 1)
                for k, (a, b) in enumerate(zip(newton, newton[1:] + [rstd[slot]])):
                    ve.wait_ge(ln_step, base + 5 + 3 * k)
                    V.scalar_tensor_tensor(yy[:], a[:], -0.5, a[:], ALU.mult, ALU.mult).then_inc(ln_step, 1)
                    ve.wait_ge(ln_step, base + 6 + 3 * k)
                    V.tensor_tensor(yy[:], yy[:], var_e[:], ALU.mult).then_inc(ln_step, 1)
                    ve.wait_ge(ln_step, base + 7 + 3 * k)
                    V.scalar_tensor_tensor(b[:], yy[:], 1.5, a[:], ALU.add, ALU.mult).then_inc(ln_step, 1)
                ve.wait_ge(ln_step, base + LN_STEPS)

            def nodes(g, n, slot):
                if isinstance(g, int) and g == 1:
                    biases()
                    phase()
                ve.wait_ge(x_in[slot], 16 * (n + 1))
                count(ve, h_ready, g - 2)
                layernorm(slot, xg[slot], g * LN_STEPS)
                V.scalar_tensor_tensor(shift[slot][:], st2[slot][:, :, 0], -1.0, rstd[slot][:], ALU.mult, ALU.mult).then_inc(nrm_ready, 1)
                if isinstance(g, int) and g == 2:
                    envelope()
                if isinstance(g, int) and g == N_GROUPS - 1:
                    small_weights()

            def biases():
                ve.wait_ge(bias_in, 64)
                V.tensor_copy(bias_bf[:, 0], bias_rows[:, 0]).then_inc(bias_step, 1)
                for k in range(2):
                    ve.wait_ge(bias_step, 2 * k + 1)
                    V.tensor_tensor(bias_rows[:, k + 1], bias_rows[:, k], bias_bf[:, k], ALU.subtract).then_inc(bias_step, 1)
                    ve.wait_ge(bias_step, 2 * k + 2)
                    V.tensor_copy(bias_bf[:, k + 1], bias_rows[:, k + 1]).then_inc(bias_step, 1)
                ve.wait_ge(bias_step, 5)
                ve.wait_ge(v_small, 3)
                for k in range(3):
                    V.tensor_copy(bias_parts[32 * k:32 * k + 1], bias_bf[32 * k:32 * k + 1, k]).then_inc(bias_step, 1)

            def small_weights():
                ve.wait_ge(wts_in, 16 * N_WTS)
                V.scalar_tensor_tensor(rw_sb[:], wid_sb[:], -1.0, wid_sb[:], ALU.mult, ALU.max).then_inc(v_small, 1)
                ve.wait_ge(v_small, 4)
                V.tensor_scalar(rw_sb[:], rw_sb[:], EPS_W, None, ALU.add).then_inc(v_small, 1)
                ve.wait_ge(v_small, 5)
                V.reciprocal(rw_sb[:], rw_sb[:]).then_inc(v_small, 1)
                V.tensor_scalar(neg_cen[:], cen_sb[:], -1.0, None, ALU.mult).then_inc(v_small, 1)
                ve.wait_ge(v_small, 6)
                V.scalar_tensor_tensor(exp_scale[:], rw_sb[:], -0.5, rw_sb[:], ALU.mult, ALU.mult).then_inc(v_small, 1)
                ve.wait_ge(fuse_mm, 1)
                V.tensor_copy(w23_sb[:], wps[1][:, 0:HID]).then_inc(fuse_v, 1)
                V.tensor_tensor(b23_sb[:], wps[1][:, HID:HID + 2], fb1_sb[:], ALU.add).then_inc(fuse_v, 1)
                ve.wait_ge(p_step, 3)
                V.tensor_copy(dump_f[:], dump_i[:]).then_inc(v_small, 1)
                ve.wait_ge(fuse_v, 2)
                for k, (whole, parts) in enumerate(((w23_sb[:], w23_p), (f2_sb, f2_p), (f3_sb, f3_p))):
                    V.tensor_copy(parts[0][:], whole).then_inc(part_ready, 1)
                    ve.wait_ge(part_ready, 2 * k + 1)
                    V.tensor_tensor(parts[1][:], whole, parts[0][:].bitcast(F32), ALU.subtract).then_inc(part_ready, 1)

            node_loop(ve, nodes, 0)
            ve.wait_ge(v_small, 9)
            ve.wait_ge(p_const, 2)
            ve.wait_ge(part_ready, 6)
            ve.wait_ge(h_ready, N_GROUPS)

            def basis(s, q):
                ve.wait_ge(exp_ready, s + 1)
                count(ve, z1_ready, s - 1)
                V.tensor_tensor(r_in[q][:], u[q][:], e_bc[q][:], ALU.mult).then_inc(r_ready, 1)

            def targets(s, n, q):
                ve.wait_ge(src_in[q], 32 * (n + 1))
                count(ve, c_ready, s * 4 - 4)
                sc = src_c[q][:]
                V.tensor_scalar(to_dump[:], sc, -1.0, dump_f[:], ALU.mult, ALU.add).then_inc(dump_ready, 1)
                for j in range(8):
                    i = V.scalar_tensor_tensor(same[q][:, j, :], src_r[q][:, j * P:(j + 1) * P], src_c[q][:, j:j + 1], upto[:],
                                               ALU.is_equal, ALU.mult, accum_out=n_upto[:, j:j + 1])
                i.then_inc(cnt_ready, 1)
                ve.wait_ge(cnt_ready, s + 1)
                ve.wait_ge(dump_ready, s + 1)
                V.scalar_tensor_tensor(is_dup[:], n_upto[:], 1.5, to_dump[:], ALU.is_gt, ALU.mult).then_inc(dup_ready, 1)
                ve.wait_ge(dup_ready, s + 1)
                for i in range(N_TAB):
                    count(ve, scat[i], (s - 1) * (16 * 8 // N_TAB))
                V.tensor_tensor(target[q][:], is_dup[:], sc, ALU.add).then_inc(tgt_ready, 1)

            def rest1(s, q):
                ve.wait_ge(a1_ready, s + 1)
                count(ve, z2_ready, s * 4 - 4)
                V.tensor_tensor(a1_p[q][1][:], a1, a1_p[q][0][:].bitcast(F32), ALU.subtract).then_inc(lo1_ready, 1)

            def rest(c, k, ready, a, a_p, read, done):
                for m in range(2):
                    ve.wait_ge(ready, c * 2 + m + 1)
                    if m == 0:
                        count(ve, read, c * 2 - 2)
                    V.tensor_tensor(a_p[k % 2][1][:, m, :], a[m], a_p[k % 2][0][:, m, :].bitcast(F32),
                                    ALU.subtract).then_inc(done, 1)

            def messages(c, n, k):
                s_half = k % 2
                q = (k % 4) // 2
                n2 = n + (k - k % 4) // 4
                def product(pair):
                    ve.wait_ge(w_ready, c * 2 + pair + 1)
                    ve.wait_ge(gath[q][s_half * 2 + pair], 32 * (n2 + 1))
                    count(ve, c_ready, c * 2 - 3 + pair)
                    V.tensor_tensor(msg[pair][:], wps[pair][:], hn_g[q][s_half * 2 + pair], ALU.mult).then_inc(msg_ready, 1)

                def high(pair):
                    ve.wait_ge(msg_ready, c * 2 + pair + 1)
                    V.tensor_copy(msg_p[s_half][pair][0][:], msg[pair][:]).then_inc(mhi_ready, 1)

                def low(pair):
                    hi, lo = msg_p[s_half][pair]
                    ve.wait_ge(mhi_ready, c * 2 + pair + 1)
                    V.tensor_tensor(lo[:], msg[pair][:], hi[:].bitcast(F32), ALU.subtract).then_inc(mlo_ready, 1)

                product(0)
                high(0)
                product(1)
                low(0)
                high(1)
                low(1)

            def step(t, n, k):
                if exists(t):
                    rest(t, k, a2_ready, a2, a2_p, z3_ready, lo2_ready)
                if k % 2 == 1 and exists(n * 2 + (k + 1) // 2, N_SUPER):
                    rest1(n * 2 + (k + 1) // 2, (k + 1) // 2 % 2)
                if k == 2 and exists(n * 2 + 2, N_SUPER):
                    for i in range(2):
                        basis(n * 2 + 2 + i, i)
                if exists(t - 1):
                    rest(t - 1, k + 1, a3_ready, a3, a3_p, w_ready, lo3_ready)
                if exists(t - 2):
                    messages(t - 2, n, k - 2)
                if k % 2 == 1:
                    s = n * 2 + k // 2
                    if exists(s, N_SUPER):
                        targets(s, n, k // 2)

            for s in range(2):
                basis(s, s)
            rest1(0, 0)
            edge_loop(ve, step, 3)

            ve.wait_ge(bc_in, 16 * N_BC)

            def last(g, n, slot):
                ve.wait_ge(fs_ready, g + 1)
                layernorm(slot, f_t0[slot], (g + N_GROUPS) * LN_STEPS)
                count(ve, out_ready, g - 2)
                for t in range(G_T):
                    i = V.scalar_tensor_tensor(f_n[slot][:, t, :], f_t0[slot][:, t, :], st2[slot][:, t, 0:1], lg_bc[:],
                                               ALU.subtract, ALU.mult)
                i.then_inc(fc_ready, 1)
                ve.wait_ge(fc_ready, g + 1)
                for t in range(G_T):
                    i = V.scalar_tensor_tensor(f_n[slot][:, t, :], f_n[slot][:, t, :], rstd[slot][:, t:t + 1], lb_bc[:],
                                               ALU.mult, ALU.add)
                i.then_inc(fn_ready, 1)

            node_loop(ve, last, 0)


_INS = ["x", "src_cols", "src_rows", "dst_cols", "dist", "centers", "widths", "w1", "b1", "w2t", "b2", "f1", "fb1",
        "f2", "fb2", "f3", "fb3", "node_w", "node_b", "ln_g", "ln_b", "gate_w", "gate_b"]


def kernel(x, src, dst, edge_weight, L0_gnn_centers, L0_gnn_widths, L0_gnn_rbf_w1, L0_gnn_rbf_b1,
           L0_gnn_rbf_w2, L0_gnn_rbf_b2, L0_gnn_filt_w1, L0_gnn_filt_b1, L0_gnn_filt_w2, L0_gnn_filt_b2,
           L0_gnn_filt_w3, L0_gnn_filt_b3, L0_gnn_node_w, L0_gnn_node_b, L0_gnn_ln_g, L0_gnn_ln_b,
           L0_gnn_gate_w, L0_gnn_gate_b):
    import concourse.bacc as bacc
    from concourse.bass_utils import run_bass_kernel_spmd

    def pad(a, n, value=0):
        a = np.asarray(a)
        return np.concatenate([a, np.full((n - a.shape[0],) + a.shape[1:], value, a.dtype)])

    def columns(a):
        return np.ascontiguousarray(a.reshape(N_SUPER, 8, TILE).transpose(0, 2, 1))

    def halves(a):
        return np.ascontiguousarray(np.asarray(a).reshape(2, P).T)

    src_p = pad(src, E_PAD, N_PAD - 1)
    dst_p = pad(dst, E_PAD, 0)
    w2t = np.asarray(L0_gnn_rbf_w2).T
    arrays = {
        "x": pad(x, N_PAD), "src_cols": columns(src_p), "src_rows": src_p, "dst_cols": columns(dst_p),
        "dist": pad(edge_weight, E_PAD), "centers": L0_gnn_centers,
        "widths": np.concatenate([np.asarray(L0_gnn_widths)] * 2).reshape(P, 1),
        "w1": L0_gnn_rbf_w1, "b1": L0_gnn_rbf_b1, "w2t": np.concatenate([w2t, w2t], axis=1), "b2": L0_gnn_rbf_b2,
        "f1": L0_gnn_filt_w1, "fb1": halves(L0_gnn_filt_b1), "f2": L0_gnn_filt_w2, "fb2": halves(L0_gnn_filt_b2),
        "f3": L0_gnn_filt_w3, "fb3": L0_gnn_filt_b3, "node_w": L0_gnn_node_w, "node_b": L0_gnn_node_b,
        "ln_g": L0_gnn_ln_g, "ln_b": L0_gnn_ln_b, "gate_w": L0_gnn_gate_w, "gate_b": L0_gnn_gate_b,
    }
    arrays = {k: np.ascontiguousarray(v) for k, v in arrays.items()}
    nc = bacc.Bacc("TRN2", target_bir_lowering=False, num_devices=1)
    args = [nc.dram_tensor(n, arrays[n].shape, mybir.dt.from_np(arrays[n].dtype), kind="ExternalInput").ap() for n in _INS]
    args.append(nc.dram_tensor("out", (N_PAD, HID), F32, kind="ExternalOutput").ap())
    build(nc, *args)
    result = run_bass_kernel_spmd(nc, [arrays], core_ids=[0])
    return result.results[0]["out"][:N_NODES]
```

```python
from contextlib import ExitStack

import numpy as np

import concourse.bass as bass
from concourse import mybir

P = 128
HID = 256
R = 64
N_NODES = 6250
N_EDGES = 100000

G_T = 5
G_ROWS = G_T * P
N_GROUPS = 10
SLOTS = 3
N_PAD = N_GROUPS * G_ROWS
DUMP = N_PAD
T_ROWS = N_PAD + P

TILE = P
CHUNK = 4 * TILE
SUPER = 2 * CHUNK
N_SUPER = -(-N_EDGES // SUPER)
N_SUPER += N_SUPER % 2
N_CHUNK = 2 * N_SUPER
E_PAD = N_SUPER * SUPER
E_COLS = E_PAD // P
N_TAB = 2

CUTOFF = 10.0
EPS_W = 1e-05
EPS_LN = 1e-05
ROUND = 1.5 * 2.0 ** 23

F32 = mybir.dt.float32
F32R = mybir.dt.float32r
BF16 = mybir.dt.bfloat16
I32 = mybir.dt.int32
ALU = mybir.AluOpType
ACT = mybir.ActivationFunctionType
AX_X = mybir.AxisListType.X


def build(nc, x, src_cols, src_rows, dst_cols, dist, centers, widths, w1, b1, w2t, b2, f1, fb1,
          f2, fb2, f3, fb3, node_w, node_b, ln_g, ln_b, gate_w, gate_b, out):
    with ExitStack() as ctx:
        def sb(name, shape, dt=F32):
            return ctx.enter_context(nc.sbuf_tensor(name, shape, dt))

        def ps(name):
            return ctx.enter_context(nc.psum_tensor(name, [P, 512], F32))

        def sem(name):
            return ctx.enter_context(nc.semaphore(name))

        hn_tab = nc.dram_tensor("hn_tab", [N_PAD, HID], F32).ap()
        agg = [nc.dram_tensor(f"agg{i}", [T_ROWS, HID], F32).ap() for i in range(N_TAB)]
        env_d = nc.dram_tensor("env_d", [E_PAD], F32).ap()

        w1_sb = sb("w1_sb", [P, P])
        w2t_sb = sb("w2t_sb", [R, P])
        f1_sb = sb("f1_sb", [R, HID])
        w23_sb = sb("w23_sb", [P, HID])
        w23_p = [sb(f"w23_p{i}", [P, HID], F32R) for i in range(2)]
        f2_p = [sb(f"f2_p{i}", [P, 2, HID], F32R) for i in range(2)]
        f3_p = [sb(f"f3_p{i}", [P, 2, HID], F32R) for i in range(2)]
        nw_sb = sb("nw_sb", [P, 2, HID])
        gw_sb = sb("gw_sb", [P, 2, HID])
        b1_sb = sb("b1_sb", [P, 1])
        b2_sb = sb("b2_sb", [R, 1])
        fb1_sb = sb("fb1_sb", [P, 2])
        b23_sb = sb("b23_sb", [P, 2])
        fb2_sb = sb("fb2_sb", [P, 2])
        bias_bf = sb("bias_bf", [96, 3, 3, HID], BF16)
        bias_parts = sb("bias_parts", [96, 3, HID], BF16)
        ones_bf = sb("ones_bf", [96, P], BF16)
        lg_bc = sb("lg_bc", [P, HID])
        lb_bc = sb("lb_bc", [P, HID])
        cen_sb = sb("cen_sb", [P, 1])
        wid_sb = sb("wid_sb", [P, 1])
        rw_sb = sb("rw_sb", [P, 1])
        neg_cen = sb("neg_cen", [P, 1])
        exp_scale = sb("exp_scale", [P, 1])
        ident = sb("ident", [P, P])
        upto = sb("upto", [P, P])
        dump_i = sb("dump_i", [P, 1], I32)
        dump_f = sb("dump_f", [P, 1])
        half_pi = sb("half_pi", [P, 1])
        stage = sb("stage", [P, 4 * E_COLS])
        dist_c = stage[:, 0:E_COLS]
        ev = [stage[:, (i + 1) * E_COLS:(i + 2) * E_COLS] for i in range(3)]
        a1 = stage[:, 0:CHUNK]
        a2 = [stage[:, (1 + m) * CHUNK:(2 + m) * CHUNK] for m in range(2)]
        a3 = [stage[:, (3 + m) * CHUNK:(4 + m) * CHUNK] for m in range(2)]

        N_ROWS = 16 * 2 * HID
        work = sb("work", [P, N_ROWS + 10 * CHUNK])
        rows = work[:, 0:N_ROWS].rearrange("p (a n) -> p a n", a=16)
        hn_g = [[rows[:, 4 * i + j, :] for j in range(4)] for i in range(2)]
        summed = [[rows[:, 8 + 4 * i + j, :] for j in range(4)] for i in range(2)]
        tail = [work[:, N_ROWS + i * CHUNK:N_ROWS + (i + 1) * CHUNK] for i in range(10)]
        d_bc = tail[0:2]
        e_bc = tail[2:4]
        u = tail[4:6]
        r_in = tail[6:8]
        msg = tail[8:10]
        f2_sb, f3_sb = [msg[i].rearrange("p (k n) -> p k n", k=2) for i in range(2)]

        G_LEN = G_T * HID
        own = sb("own", [P, (SLOTS + 1) * G_LEN])
        x_sb = sb("x_sb", [P, SLOTS * G_LEN])

        def groups(t, first, n=SLOTS, at=0):
            return [t[:, at + i * G_LEN:at + (i + 1) * G_LEN].rearrange("p (t h) -> p t h", t=G_T) for i in range(first, first + n)]

        xg = groups(x_sb, 0)
        hT = groups(work, 0)
        og = groups(work, SLOTS)
        hg = groups(own, 0)
        zeros = groups(own, SLOTS, 1)[0]
        bias_rows = work[0:96, N_ROWS:N_ROWS + 9 * HID].rearrange("p (k b n) -> p k b n", k=3, b=3)
        f_t = groups(work, 0)
        f_n = groups(own, 0)
        f_x = groups(x_sb, 0)
        f_o = groups(work, 2 * SLOTS)
        f_T = groups(work, 3 * SLOTS, 1) + groups(stage, 0, 2)
        st6 = sb("st6", [P, G_T, 6])
        st2 = [sb(f"st2{i}", [P, G_T, 2]) for i in range(SLOTS)]
        var_e = sb("var_e", [P, G_T])
        seed = sb("seed", [P, G_T], I32)
        yy = sb("yy", [P, G_T])
        newton = [sb(f"newton{i}", [P, G_T]) for i in range(3)]
        rstd = [sb(f"rstd{i}", [P, G_T]) for i in range(SLOTS)]
        shift = [sb(f"shift{i}", [P, G_T]) for i in range(SLOTS)]

        src_r = [sb(f"src_r{i}", [P, SUPER], I32) for i in range(2)]
        src_c = [sb(f"src_c{i}", [P, 8], I32) for i in range(2)]
        dst_c = [sb(f"dst_c{i}", [P, 8], I32) for i in range(2)]
        a1_p = [[sb(f"a1_p{i}{j}", [P, CHUNK], F32R) for j in range(2)] for i in range(2)]
        same = [sb(f"same{i}", [P, 8, P], F32R) for i in range(2)]
        n_upto = sb("n_upto", [P, 8])
        is_dup = sb("is_dup", [P, 8])
        to_dump = sb("to_dump", [P, 8])
        target = [sb(f"target{i}", [P, 8], I32) for i in range(2)]
        a2_p = [[sb(f"a2_p{i}{j}", [P, 2, CHUNK], F32R) for j in range(2)] for i in range(2)]
        a3_p = [[sb(f"a3_p{i}{j}", [P, 2, CHUNK], F32R) for j in range(2)] for i in range(2)]
        msg_p = [[[sb(f"msg_p{i}{j}{k}", [P, 2 * HID], F32R) for k in range(2)] for j in range(2)] for i in range(2)]

        z1 = ps("z1")
        z2 = [ps("z2a"), ps("z2b")]
        z3 = [ps("z3a"), ps("z3b")]
        wps = [ps("wa"), ps("wb")]
        cps = [ps("cps"), z1]

        w1_clear = sem("w1_clear")
        wts_in = sem("wts_in")
        bc_in = sem("bc_in")
        dist_in = sem("dist_in")
        p_step = sem("p_step")
        pool_pass = sem("pool_pass")
        ve_pass = sem("ve_pass")
        p_const = sem("p_const")
        x_in = [sem(f"x_in{i}") for i in range(SLOTS)]
        hn_free = [sem(f"hn_free{i}") for i in range(SLOTS)]
        h_out = [sem(f"h_out{i}") for i in range(SLOTS)]
        zeroed = sem("zeroed")
        v_env = sem("v_env")
        a_env = sem("a_env")
        env_ok = sem("env_ok")
        env_out = sem("env_out")
        fuse_mm = sem("fuse_mm")
        fuse_v = sem("fuse_v")
        bias_step = sem("bias_step")
        bias_in = sem("bias_in")
        v_small = sem("v_small")
        ln_step = sem("ln_step")
        nrm_ready = sem("nrm_ready")
        h_ready = sem("h_ready")
        t_ready = sem("t_ready")
        hT_ready = sem("hT_ready")
        np_ready = sem("np_ready")
        hn_ready = sem("hn_ready")
        tab_in = [sem(f"tab_in{i}") for i in range(SLOTS)]
        fx_in = [sem(f"fx_in{i}") for i in range(SLOTS)]
        sum_in = [sem(f"sum_in{i}") for i in range(SLOTS)]
        fc_ready = sem("fc_ready")
        fn_ready = sem("fn_ready")
        ft_ready = sem("ft_ready")
        fnT_ready = sem("fnT_ready")
        gp_ready = sem("gp_ready")
        sg_ready = sem("sg_ready")
        fg_ready = sem("fg_ready")
        out_ready = sem("out_ready")
        out_free = [sem(f"out_free{i}") for i in range(SLOTS)]

        d_in = [sem("d_in0"), sem("d_in1")]
        dst_in = [sem("dst_in0"), sem("dst_in1")]
        src_in = [sem("src_in0"), sem("src_in1")]
        gath = [[sem(f"gath{i}_{j}") for j in range(4)] for i in range(2)]
        scat = [sem(f"scat{i}") for i in range(N_TAB)]
        sq_ready = sem("sq_ready")
        exp_ready = sem("exp_ready")
        r_ready = sem("r_ready")
        z1_ready = sem("z1_ready")
        a1_ready = sem("a1_ready")
        z2_ready = sem("z2_ready")
        a2_ready = sem("a2_ready")
        z3_ready = sem("z3_ready")
        a3_ready = sem("a3_ready")
        lo1_ready = sem("lo1_ready")
        lo2_ready = sem("lo2_ready")
        lo3_ready = sem("lo3_ready")
        part_ready = sem("part_ready")
        w_ready = sem("w_ready")
        msg_ready = sem("msg_ready")
        mhi_ready = sem("mhi_ready")
        mlo_ready = sem("mlo_ready")
        cnt_ready = sem("cnt_ready")
        dup_ready = sem("dup_ready")
        dump_ready = sem("dump_ready")
        tgt_ready = sem("tgt_ready")
        c_ready = sem("c_ready")
        sum_ready = sem("sum_ready")

        N_WTS = 15
        N_BC = 2
        SLOT_USES = [len(range(i, N_GROUPS, SLOTS)) for i in range(SLOTS)]
        LN_STEPS = 14
        x_v = x.rearrange("(g p t) h -> g p t h", p=P, t=G_T)
        out_v = out.rearrange("(g p t) h -> g p t h", p=P, t=G_T)
        hn_v = hn_tab.rearrange("(g p t) h -> g p t h", p=P, t=G_T)
        agg_v = [a[0:N_PAD, :].rearrange("(g p t) h -> g p t h", p=P, t=G_T) for a in agg]
        dist_ch = dist.rearrange("(c a e) -> c a e", a=1, e=CHUNK)
        env_ch = env_d.rearrange("(c a e) -> c a e", a=1, e=CHUNK)
        srow_v = src_rows.rearrange("(s a e) -> s a e", a=1, e=SUPER)

        def row(v, n=P):
            return v.rearrange("(a n) -> a n", a=1).to_broadcast([n, v.shape[0]])

        def col(v):
            return v.rearrange("(n a) -> n a", a=1)

        def wait_past(engine, semaphore, n):
            if not isinstance(n, int) or n > 0:
                engine.wait_ge(semaphore, n)

        def node_loop(eng, step, extra):
            for g in range(SLOTS):
                step(g, g // SLOTS, g % SLOTS)
            with eng.Fori(1, N_GROUPS // SLOTS) as it:
                for slot in range(SLOTS):
                    step(it * SLOTS + slot, it, slot)
            for g in range(N_GROUPS // SLOTS * SLOTS, N_GROUPS + extra):
                step(g, g // SLOTS, g % SLOTS)

        def before(n, slot, d):
            return n + (slot - d) // SLOTS, (slot - d) % SLOTS

        def edge_loop(eng, step, extra):
            for t in range(8):
                step(t, t // 4, t % 4)
            with eng.Fori(2, N_CHUNK // 4 - 1) as it:
                for k in range(4):
                    step(it * 4 + k, it, k)
            for t in range(N_CHUNK - 4, N_CHUNK + extra):
                step(t, t // 4, t % 4)

        TERMS = ((0, 0), (0, 1), (1, 0))

        def exists(c, last=N_CHUNK):
            return not isinstance(c, int) or 0 <= c < last

        block = ctx.enter_context(nc.Block())

        @block.sync
        def _(sp):
            def dst_of(s, n, q):
                for j in range(4):
                    wait_past(sp, gath[q][j], 32 * n)
                sp.dma_start(dst_c[q][:], dst_cols[s]).then_inc(dst_in[q], 16)

            def src_of(s, q):
                wait_past(sp, tgt_ready, s - 1)
                sp.dma_start(src_r[q][:], srow_v[s].to_broadcast([P, SUPER])).then_inc(src_in[q], 16)
                sp.dma_start(src_c[q][:], src_cols[s]).then_inc(src_in[q], 16)

            def weights():
                sp.wait_ge(w1_clear, 1)
                for dst, src in ((w1_sb[0:R, 0:R], w1), (w1_sb[R:P, R:P], w1),
                                 (w2t_sb[:], w2t), (f1_sb[:], f1),
                                 (f2_sb, f2.rearrange("(k p) n -> p k n", p=P)),
                                 (f3_sb, f3.rearrange("(k p) n -> p k n", p=P)),
                                 (gw_sb[:], gate_w.rearrange("(k p) n -> p k n", p=P)),
                                 (b1_sb[0:R, :], col(b1)), (b1_sb[R:P, :], col(b1)),
                                 (b2_sb[:], col(b2)),
                                 (fb1_sb[:], fb1), (fb2_sb[:], fb2),
                                 (cen_sb[0:R, :], col(centers)), (cen_sb[R:P, :], col(centers)),
                                 (wid_sb[:], widths)):
                    sp.dma_start(dst, src).then_inc(wts_in, 16)
                for dst, src in ((lg_bc[:], ln_g), (lb_bc[:], ln_b)):
                    sp.dma_start(dst, row(src)).then_inc(bc_in, 16)

            def distances(s, q):
                wait_past(sp, r_ready, s - 1)
                for half in range(2):
                    part = slice(half * R, half * R + R)
                    sp.dma_start(d_bc[q][part, :], dist_ch[s * 2 + half].to_broadcast([R, CHUNK])).then_inc(d_in[q], 16)
                    sp.dma_start(e_bc[q][part, :], env_ch[s * 2 + half].to_broadcast([R, CHUNK])).then_inc(d_in[q], 16)

            def nodes(g, n, slot):
                if exists(g, N_GROUPS):
                    wait_past(sp, h_ready, g - 2)
                    sp.dma_start(xg[slot], x_v[g]).then_inc(x_in[slot], 16)
                if isinstance(g, int) and g == 1:
                    sp.dma_start(dist_c, dist.rearrange("(p c) -> p c", p=P)).then_inc(dist_in, 16)
                if isinstance(g, int) and g == 2:
                    weights()
                if isinstance(g, int) and g == N_GROUPS - 1:
                    for q in range(2):
                        dst_of(q, 0, q)
                        src_of(q, q)
                    sp.wait_ge(env_ok, 1)
                    sp.dma_start(env_d.rearrange("(p c) -> p c", p=P), ev[0]).then_inc(env_out, 16)
                if exists(g - 1, N_GROUPS):
                    if isinstance(g, int) and g == N_GROUPS:
                        sp.wait_ge(env_out, 16)
                        for s in range(2):
                            distances(s, s)
                    sp.wait_ge(h_ready, g)
                    sp.dma_start(agg_v[0][g - 1], hg[(slot - 1) % SLOTS]).then_inc(h_out[(slot - 1) % SLOTS], 16)

            node_loop(sp, nodes, 1)

            def two(n, more=True):
                dst_of(n * 2, n, 0)
                if more:
                    for q in range(2):
                        distances(n * 2 + 2 + q, q)
                src_of(n * 2, 0)
                dst_of(n * 2 + 1, n, 1)
                src_of(n * 2 + 1, 1)

            for s in range(2, 4):
                distances(s, s % 2)
            with sp.Fori(1, N_SUPER // 2 - 1) as it:
                two(it)
            two(N_SUPER // 2 - 1, more=False)

            for i in range(N_TAB):
                sp.wait_ge(scat[i], 16 * N_SUPER * 8 // N_TAB)
            sp.wait_ge(sum_ready, 2 * N_CHUNK)

            def last(g, n, slot):
                wait_past(sp, fn_ready, g - 2)
                sp.dma_start(f_t[slot], agg_v[0][g]).then_inc(tab_in[slot], 16)

            node_loop(sp, last, 0)
            for i in range(SLOTS):
                sp.wait_ge(out_free[i], 16 * (SLOT_USES[i] + 1))

        @block.gpsimd
        def _(pool):
            pool.memset(w1_sb[:], 0.0).then_inc(w1_clear, 1)
            pool.memset(ident[:], 0.0).then_inc(p_step, 1)
            pool.memset(upto[:], 1.0).then_inc(p_step, 1)
            pool.iota(dump_i[:], pattern=[[0, 1]], base=DUMP, channel_multiplier=1).then_inc(p_step, 1)
            pool.memset(zeros, 0.0).then_inc(p_step, 1)
            pool.wait_ge(p_step, 4)
            pool.affine_select(out=ident[:], in_=ident[:], compare_op=ALU.not_equal, fill=1.0,
                               base=0, pattern=[[-1, P]], channel_multiplier=1).then_inc(p_const, 1)
            pool.affine_select(out=upto[:], in_=upto[:], compare_op=ALU.is_ge, fill=0.0,
                               base=0, pattern=[[-1, P]], channel_multiplier=1).then_inc(p_const, 1)
            for i in range(N_TAB):
                pool.dma_start(agg[i][DUMP:T_ROWS, :], zeros[:, 0, :]).then_inc(zeroed, 16)

            def clear(g):
                for i in range(1, N_TAB):
                    pool.dma_start(agg_v[i][g], zeros).then_inc(zeroed, 16)

            N_EARLY = N_GROUPS * 4 // 10
            for g in range(N_EARLY):
                pool.wait_ge(h_ready, g + 1)
                clear(g)

            for i in range(SLOTS):
                pool.wait_ge(hn_free[i], 16 * (SLOT_USES[i] + 1))

            def gather(s, n, q, j):
                pool.indirect_dma_start(
                    out=hn_g[q][j // 2][:, (j % 2) * HID:(j % 2 + 1) * HID], out_offset=None, in_=hn_tab,
                    in_offset=bass.IndirectOffsetOnAxis(ap=dst_c[q][:, j:j + 1], axis=0),
                ).then_inc(gath[q][j // 2], 16)

            def scatter(s, n, q, j):
                i = j % N_TAB
                per = 8 // N_TAB
                if j % 2 == 0:
                    pool.wait_ge(sum_ready, s * 4 + j // 2 + 1)
                if j == 0:
                    pool.wait_ge(tgt_ready, s + 1)
                if isinstance(s, int) and s + j == 0:
                    pool.wait_ge(zeroed, 16 * (N_TAB + (N_TAB - 1) * N_GROUPS))
                    for i2 in range(SLOTS):
                        pool.wait_ge(h_out[i2], 16 * SLOT_USES[i2])
                wait_past(pool, scat[i], (s * per + j // N_TAB) * 16)
                if not isinstance(s, int):
                    pool.sem_inc(pool_pass, 1)
                pool.indirect_dma_start(
                    out=agg[i], out_offset=bass.IndirectOffsetOnAxis(ap=target[q][:, j:j + 1], axis=0),
                    in_=summed[q][j // 2][:, (j % 2) * HID:(j % 2 + 1) * HID], in_offset=None, compute_op=ALU.add,
                ).then_inc(scat[i], 16)

            def superchunk(s, n, q):
                if exists(s, N_SUPER):
                    pool.wait_ge(dst_in[q], 16 * (n + 1))
                for j in range(8):
                    if exists(s, N_SUPER):
                        if j % 2 == 0:
                            wait_past(pool, msg_ready, s * 4 - 8 + j // 2 + 1)
                            if not isinstance(s, int):
                                pool.sem_inc(pool_pass, 1)
                        gather(s, n, q, j)
                    if exists(s - 2, N_SUPER):
                        scatter(s - 2, n - 1, q, j)

            for s in range(2):
                superchunk(s, s // 2, s % 2)
            for g in range(N_EARLY, N_GROUPS):
                clear(g)
            for s in range(2, 4):
                superchunk(s, s // 2, s % 2)
            with pool.Fori(2, N_SUPER // 2) as it:
                for q in range(2):
                    superchunk(it * 2 + q, it, q)
            for s in range(N_SUPER, N_SUPER + 2):
                superchunk(s, s // 2, s % 2)

            def last(g, n, slot):
                if exists(g, N_GROUPS):
                    pool.wait_ge(tab_in[slot], 16 * (n + 1))
                    pool.dma_start(f_t[slot], agg_v[1][g], accum_op=ALU.add).then_inc(sum_in[slot], 16)
                if exists(g - 3, N_GROUPS - 1):
                    n3, slot3 = before(n, slot, 3)
                    pool.wait_ge(sg_ready, (g - 2) * 3)
                    pool.tensor_tensor(f_o[slot3], f_o[slot3], f_n[slot3], ALU.mult).then_inc(fg_ready, 1)
                    pool.wait_ge(fx_in[slot3], 16 * (n3 + 1))
                    pool.wait_ge(fg_ready, g - 2)
                    pool.tensor_tensor(f_o[slot3], f_o[slot3], f_x[slot3], ALU.add).then_inc(out_ready, 1)

            node_loop(pool, last, 2)

        @block.scalar
        def _(act):
            def transposed(g, T, ready, used, done):
                act.wait_ge(ready, g + 1)
                wait_past(act, used, g - 2)
                flat = T.rearrange("p t h -> p (t h)")
                for b, bank in enumerate((z1, z2[0], z2[1])):
                    n = min(512, G_LEN - 512 * b)
                    i = act.activation(flat[:, 512 * b:512 * b + n], bank[:, 0:n], ACT.Copy)
                i.then_inc(done, 1)

            def first_weights():
                for k, v in enumerate((fb3, node_b, gate_b)):
                    act.dma_start(bias_rows[:, 0, k, :], row(v, 96)).then_inc(bias_in, 16)
                act.dma_start(nw_sb[:], node_w.rearrange("(k p) n -> p k n", p=P)).then_inc(bias_in, 16)

            def squares(s0, n):
                for q in range(2):
                    act.wait_ge(d_in[q], 64 * (n + 1))
                    wait_past(act, r_ready, s0 + q - 1)
                    act.activation(u[q], d_bc[q], ACT.Square, bias=neg_cen[:]).then_inc(sq_ready, 1)

            def exps(s0):
                for q in range(2):
                    act.wait_ge(sq_ready, s0 + q + 1)
                    act.activation(u[q], u[q], ACT.Exp, scale=exp_scale[:]).then_inc(exp_ready, 1)

            def nodes(g, n, slot):
                if exists(g, N_GROUPS):
                    act.wait_ge(nrm_ready, g + 1)
                    wait_past(act, t_ready, g - 2)
                    wait_past(act, h_out[slot], 16 * n)
                    for t in range(G_T):
                        i = act.activation(hg[slot][:, t, :], xg[slot][:, t, :], ACT.Relu,
                                           bias=shift[slot][:, t:t + 1], scale=rstd[slot][:, t:t + 1])
                    i.then_inc(h_ready, 1)
                if exists(g - 2, N_GROUPS):
                    if isinstance(g, int) and g == N_GROUPS + 1:
                        act.wait_ge(v_small, 9)
                        squares(0, 0)
                        exps(0)
                    n2, slot2 = before(n, slot, 2)
                    flat = og[slot2].rearrange("p t h -> p (t h)")
                    act.wait_ge(np_ready, g - 1)
                    act.wait_ge(hn_free[slot2], 16 * (n2 + 1))
                    for b, bank in enumerate((z3[0], z3[1], wps[0])):
                        w = min(512, G_LEN - 512 * b)
                        act.activation(flat[:, 512 * b:512 * b + w], bank[:, 0:w], ACT.Copy).then_inc(hn_ready, 1)
                    act.wait_ge(hn_ready, (g - 1) * 3)
                    act.dma_start(hn_v[g - 2], og[slot2]).then_inc(hn_free[slot2], 16)
                if exists(g, N_GROUPS):
                    transposed(g, hT[slot], t_ready, np_ready, hT_ready)
                if isinstance(g, int) and g == 2:
                    act.wait_ge(v_small, 1)
                    act.wait_ge(v_env, 4)
                    act.activation(ev[1], ev[0], ACT.Sin, bias=half_pi[:], scale=-2.0 * np.pi).then_inc(a_env, 1)

            first_weights()
            for free in hn_free + out_free:
                act.sem_inc(free, 16)
            node_loop(act, nodes, 2)

            def silu1(s, q):
                act.wait_ge(z1_ready, s + 1)
                wait_past(act, z2_ready, s * 4 - 4)
                wait_past(act, lo1_ready, s)
                act.activation(a1, z1[:], ACT.Silu, bias=b1_sb[:])
                act.activation(a1_p[q][0][:], z1[:], ACT.Silu, bias=b1_sb[:]).then_inc(a1_ready, 1)

            def step(t, n, k):
                if exists(t):
                    for m in range(2):
                        act.wait_ge(z2_ready, t * 2 + m + 1)
                        if m == 0:
                            wait_past(act, z3_ready, t * 2 - 2)
                        wait_past(act, lo2_ready, t * 2 - 1 + m)
                        act.activation(a2[m], z2[m][:], ACT.Silu, bias=b23_sb[:, m:m + 1])
                        act.activation(a2_p[k % 2][0][:, m, :], z2[m][:], ACT.Silu, bias=b23_sb[:, m:m + 1]).then_inc(a2_ready, 1)
                if k % 2 == 1:
                    s = n * 2 + (k + 1) // 2
                    if exists(s, N_SUPER):
                        silu1(s, (k + 1) // 2 % 2)
                c = t - 3
                q = ((k + 1) // 2) % 2

                def take_sums(pair):
                    if exists(c):
                        act.wait_ge(c_ready, c * 2 + pair + 1)
                        h = (k + 1) % 2
                        slot = 2 * h + pair
                        for i in range(N_TAB):
                            wait_past(act, scat[i], (c * 2 + pair - 7) * (32 // N_TAB))
                        act.activation(summed[q][slot], cps[pair][:], ACT.Copy).then_inc(sum_ready, 1)

                if exists(t - 1):
                    for m in range(2):
                        act.wait_ge(z3_ready, (t - 1) * 2 + m + 1)
                        if m == 0:
                            wait_past(act, w_ready, t * 2 - 4)
                        wait_past(act, lo3_ready, t * 2 - 3 + m)
                        act.activation(a3[m], z3[m][:], ACT.Silu, bias=fb2_sb[:, m:m + 1])
                        act.activation(a3_p[(k + 1) % 2][0][:, m, :], z3[m][:], ACT.Silu, bias=fb2_sb[:, m:m + 1]).then_inc(a3_ready, 1)
                if k == 0 and exists(n * 2 + 2, N_SUPER):
                    squares(n * 2 + 2, n + 1)
                if k == 1 and exists(n * 2 + 2, N_SUPER):
                    exps(n * 2 + 2)
                for pair in range(2):
                    take_sums(pair)

            silu1(0, 0)
            edge_loop(act, step, 3)

            def last(g, n, slot):
                if exists(g - 1, N_GROUPS):
                    n1, slot1 = before(n, slot, 1)
                    flat = f_o[slot1].rearrange("p t h -> p (t h)")
                    act.wait_ge(gp_ready, g)
                    act.wait_ge(out_free[slot1], 16 * (n1 + 1))
                    for b, bank in enumerate((z3[0], z3[1], wps[0])):
                        w = min(512, G_LEN - 512 * b)
                        act.activation(flat[:, 512 * b:512 * b + w], bank[:, 0:w], ACT.Sigmoid).then_inc(sg_ready, 1)
                if exists(g, N_GROUPS):
                    transposed(g, f_T[slot], ft_ready, gp_ready, fnT_ready)
                if exists(g - 3, N_GROUPS):
                    slot3 = before(n, slot, 3)[1]
                    act.wait_ge(out_ready, g - 2)
                    act.dma_start(out_v[g - 3], f_o[slot3]).then_inc(out_free[slot3], 16)
                if exists(g, N_GROUPS):
                    act.dma_start(f_x[slot], x_v[g]).then_inc(fx_in[slot], 16)

            node_loop(act, last, 3)

        @block.tensor
        def _(pe):
            def fuse():
                pe.wait_ge(wts_in, 16 * N_WTS)
                nc.tensor.matmul(wps[1][:, 0:HID], w2t_sb[:], f1_sb[:], start=True, stop=True)
                for m in range(2):
                    i = nc.tensor.matmul(wps[1][:, HID + m:HID + m + 1], f1_sb[:, m * P:(m + 1) * P], b2_sb[:], start=True, stop=True)
                i.then_inc(fuse_mm, 1)

            pe.wait_ge(p_const, 2)

            def transposes(g, slot, rows_g, ready, tr, trT):
                if exists(g, N_GROUPS):
                    pe.wait_ge(ready, g + 1)
                    wait_past(pe, trT, g)
                    for b in range(2 * G_T):
                        bank = (z1, z2[0], z2[1])[b // 4]
                        i = nc.tensor.transpose(bank[:, (b % 4) * P:(b % 4 + 1) * P],
                                                rows_g[slot][:, b // 2, (b % 2) * P:(b % 2 + 1) * P], ident[:])
                    i.then_inc(tr, 1)

            def products(g, slot, T, trT, prod, prod_used, w, bias):
                if exists(g - 1, N_GROUPS):
                    pe.wait_ge(trT, g)
                    T_g = T[(slot - 1) % SLOTS]
                    for t in range(G_T):
                        if t % 2 == 0:
                            wait_past(pe, prod_used, (g - 2) * 3 + t // 2 + 1)
                        o = (z3[0], z3[1], wps[0])[t // 2][:, (t % 2) * HID:(t % 2 + 1) * HID]
                        nc.tensor.matmul(o, ones_bf[:], bias_parts[:, bias, :], start=True, stop=False)
                        for kk in range(2):
                            i = nc.tensor.matmul(o, T_g[:, t, kk * P:(kk + 1) * P], w[:, kk, :], start=False, stop=kk == 1)
                    i.then_inc(prod, 1)

            def nodes(g, n, slot):
                if isinstance(g, int) and g == 1:
                    pe.wait_ge(bias_in, 64)
                    pe.wait_ge(bias_step, 8)
                if isinstance(g, int) and g == N_GROUPS - 1:
                    fuse()
                transposes(g, slot, hg, h_ready, t_ready, hT_ready)
                products(g, slot, hT, hT_ready, np_ready, hn_ready, nw_sb, 1)

            node_loop(pe, nodes, 1)

            def layer1(s, q):
                pe.wait_ge(r_ready, s + 1)
                if isinstance(s, int) and s == 0:
                    pe.wait_ge(hT_ready, N_GROUPS)
                wait_past(pe, sum_ready, s * 4 - 8)
                nc.tensor.matmul(z1[:], w1_sb[:], r_in[q][:], start=True, stop=True).then_inc(z1_ready, 1)

            def step(t, n, k):
                if exists(t):
                    h = k % 2
                    part = slice(h * R, h * R + R)
                    q = k // 2
                    if h == 0:
                        pe.wait_ge(a1_ready, n * 2 + q + 1)
                        pe.wait_ge(lo1_ready, n * 2 + q + 1)
                    for m in range(2):
                        wait_past(pe, a2_ready, t * 2 - 1 + m)
                        for term, (wi, ai) in enumerate(TERMS):
                            i = nc.tensor.matmul(z2[m][:], w23_p[wi][part, m * P:(m + 1) * P], a1_p[q][ai][part, :],
                                                 start=term == 0, stop=term == 2)
                        i.then_inc(z2_ready, 1)
                if k % 2 == 1:
                    s = n * 2 + (k + 1) // 2
                    if exists(s, N_SUPER):
                        layer1(s, (k + 1) // 2 % 2)
                c = t - 3
                q3 = ((k + 1) // 2) % 2
                h3 = (k + 1) % 2

                def add_equal(pair):
                    if not exists(c):
                        return
                    pe.wait_ge(mlo_ready, c * 2 + pair + 1)
                    if pair == 0 and h3 == 0:
                        pe.wait_ge(cnt_ready, n * 2 + (k + 1) // 2 - 1)
                    wait_past(pe, sum_ready, c * 2 - 1 + pair)
                    if pair == 1 and k % 2 == 1 and exists(n * 2 + (k + 1) // 2, N_SUPER):
                        pe.wait_ge(a1_ready, n * 2 + (k + 1) // 2 + 1)
                    for i2 in range(2):
                        part = slice(i2 * HID, (i2 + 1) * HID)
                        for term in range(2):
                            i = nc.tensor.matmul(cps[pair][:, part], same[q3][:, h3 * 4 + pair * 2 + i2, :],
                                                 msg_p[h3][pair][term][:, part], start=term == 0, stop=term == 1)
                    i.then_inc(c_ready, 1)

                if exists(t - 1):
                    c1 = (k + 1) % 2
                    pe.wait_ge(a2_ready, t * 2)
                    pe.wait_ge(lo2_ready, t * 2)
                    for m in range(2):
                        wait_past(pe, a3_ready, t * 2 - 3 + m)
                        for kk in range(2):
                            for term, (wi, ai) in enumerate(TERMS):
                                i = nc.tensor.matmul(z3[m][:], f2_p[wi][:, kk, m * P:(m + 1) * P], a2_p[c1][ai][:, kk, :],
                                                     start=kk + term == 0, stop=kk + term == 3)
                        i.then_inc(z3_ready, 1)
                c2 = k % 2
                for pair in range(2):
                    add_equal(pair)
                    if exists(t - 2):
                        if pair == 0:
                            pe.wait_ge(a3_ready, t * 2 - 2)
                            pe.wait_ge(lo3_ready, t * 2 - 2)
                        wait_past(pe, msg_ready, t * 2 - 5 + pair)
                        for i2 in range(2):
                            tile = pair * 2 + i2
                            o = wps[pair][:, i2 * HID:(i2 + 1) * HID]
                            nc.tensor.matmul(o, ones_bf[:], bias_parts[:, 0, :], start=True, stop=False)
                            for kk in range(2):
                                for term, (ai, wi) in enumerate(TERMS):
                                    i = nc.tensor.matmul(o, a3_p[c2][ai][:, kk, tile * P:(tile + 1) * P], f3_p[wi][:, kk, :],
                                                         start=False, stop=kk + term == 3)
                        i.then_inc(w_ready, 1)

            layer1(0, 0)
            pe.wait_ge(hn_ready, 3 * N_GROUPS)
            pe.wait_ge(part_ready, 6)
            edge_loop(pe, step, 3)
            pe.wait_ge(sum_ready, 2 * N_CHUNK)

            def last(g, n, slot):
                products(g, slot, f_T, fnT_ready, gp_ready, sg_ready, gw_sb, 2)
                transposes(g, slot, f_n, fn_ready, ft_ready, fnT_ready)

            node_loop(pe, last, 1)

        @block.vector
        def _(ve):
            V = nc.vector
            V.memset(half_pi[:], 0.5 * np.pi).then_inc(v_small, 1)
            V.memset(ones_bf[:], 1.0).then_inc(v_small, 1)
            V.memset(bias_parts[:], 0.0).then_inc(v_small, 1)

            def phase():
                ve.wait_ge(dist_in, 16)
                V.tensor_scalar(ev[0], dist_c, 0.5 / CUTOFF, ROUND, ALU.mult, ALU.add).then_inc(v_env, 1)
                ve.wait_ge(v_env, 1)
                V.tensor_scalar(ev[1], ev[0], -ROUND, None, ALU.add).then_inc(v_env, 1)
                ve.wait_ge(v_env, 2)
                V.scalar_tensor_tensor(ev[2], dist_c, 0.5 / CUTOFF, ev[1], ALU.mult, ALU.subtract).then_inc(v_env, 1)
                ve.wait_ge(v_env, 3)
                V.scalar_tensor_tensor(ev[0], ev[2], -1.0, ev[2], ALU.mult, ALU.max).then_inc(v_env, 1)
                ve.wait_ge(v_env, 4)
                V.tensor_scalar(ev[2], dist_c, CUTOFF, 0.5, ALU.is_lt, ALU.mult).then_inc(v_env, 1)

            def envelope():
                ve.wait_ge(a_env, 1)
                ve.wait_ge(v_env, 5)
                V.scalar_tensor_tensor(ev[0], ev[1], 1.0, ev[2], ALU.add, ALU.mult).then_inc(env_ok, 1)

            def layernorm(slot, src, base, centre=None):
                for t in range(G_T):
                    i = V.bn_stats(st6[:, t, :], src[:, t, :])
                i.then_inc(ln_step, 1)
                ve.wait_ge(ln_step, base + 1)
                ve.sem_inc(ve_pass, 1)
                for t in range(G_T):
                    i = V.bn_aggr(st2[slot][:, t, :], st6[:, t, :])
                i.then_inc(ln_step, 1)
                ve.wait_ge(ln_step, base + 2)
                V.tensor_scalar(var_e[:], st2[slot][:, :, 1], EPS_LN, None, ALU.add).then_inc(ln_step, 1)
                if centre:
                    centre(0)
                ve.wait_ge(ln_step, base + 3)
                V.tensor_scalar(seed[:], var_e[:].bitcast(I32), 1, None, ALU.logical_shift_right).then_inc(ln_step, 1)
                if centre:
                    centre(1)
                ve.wait_ge(ln_step, base + 4)
                V.tensor_scalar(newton[0][:].bitcast(I32), seed[:], -1.0, float(0x5F3759DF), ALU.mult, ALU.add).then_inc(ln_step, 1)
                for k, (a, b) in enumerate(zip(newton, newton[1:] + [rstd[slot]])):
                    if centre:
                        centre(2 + k)
                    ve.wait_ge(ln_step, base + 5 + 3 * k)
                    V.scalar_tensor_tensor(yy[:], a[:], -0.5, a[:], ALU.mult, ALU.mult).then_inc(ln_step, 1)
                    ve.wait_ge(ln_step, base + 6 + 3 * k)
                    V.tensor_tensor(yy[:], yy[:], var_e[:], ALU.mult).then_inc(ln_step, 1)
                    ve.wait_ge(ln_step, base + 7 + 3 * k)
                    V.scalar_tensor_tensor(b[:], yy[:], 1.5, a[:], ALU.add, ALU.mult).then_inc(ln_step, 1)
                ve.wait_ge(ln_step, base + LN_STEPS)

            def nodes(g, n, slot):
                if isinstance(g, int) and g == N_GROUPS - 1:
                    envelope()
                ve.wait_ge(x_in[slot], 16 * (n + 1))
                wait_past(ve, h_ready, g - 2)
                layernorm(slot, xg[slot], g * LN_STEPS)
                V.scalar_tensor_tensor(shift[slot][:], st2[slot][:, :, 0], -1.0, rstd[slot][:], ALU.mult, ALU.mult).then_inc(nrm_ready, 1)
                if isinstance(g, int) and g == 1:
                    biases()
                if isinstance(g, int) and g == 2:
                    phase()
                if isinstance(g, int) and g == N_GROUPS - 1:
                    small_weights()

            def biases():
                ve.wait_ge(bias_in, 64)
                V.tensor_copy(bias_bf[:, 0], bias_rows[:, 0]).then_inc(bias_step, 1)
                for k in range(2):
                    ve.wait_ge(bias_step, 2 * k + 1)
                    V.tensor_tensor(bias_rows[:, k + 1], bias_rows[:, k], bias_bf[:, k], ALU.subtract).then_inc(bias_step, 1)
                    ve.wait_ge(bias_step, 2 * k + 2)
                    V.tensor_copy(bias_bf[:, k + 1], bias_rows[:, k + 1]).then_inc(bias_step, 1)
                ve.wait_ge(bias_step, 5)
                ve.wait_ge(v_small, 3)
                for k in range(3):
                    V.tensor_copy(bias_parts[32 * k:32 * k + 1], bias_bf[32 * k:32 * k + 1, k]).then_inc(bias_step, 1)

            def small_weights():
                ve.wait_ge(wts_in, 16 * N_WTS)
                V.scalar_tensor_tensor(rw_sb[:], wid_sb[:], -1.0, wid_sb[:], ALU.mult, ALU.max).then_inc(v_small, 1)
                ve.wait_ge(v_small, 4)
                V.tensor_scalar(rw_sb[:], rw_sb[:], EPS_W, None, ALU.add).then_inc(v_small, 1)
                ve.wait_ge(v_small, 5)
                V.reciprocal(rw_sb[:], rw_sb[:]).then_inc(v_small, 1)
                V.tensor_scalar(neg_cen[:], cen_sb[:], -1.0, None, ALU.mult).then_inc(v_small, 1)
                ve.wait_ge(v_small, 6)
                V.scalar_tensor_tensor(exp_scale[:], rw_sb[:], -0.5, rw_sb[:], ALU.mult, ALU.mult).then_inc(v_small, 1)
                ve.wait_ge(fuse_mm, 1)
                V.tensor_copy(w23_sb[:], wps[1][:, 0:HID]).then_inc(fuse_v, 1)
                V.tensor_tensor(b23_sb[:], wps[1][:, HID:HID + 2], fb1_sb[:], ALU.add).then_inc(fuse_v, 1)
                ve.wait_ge(p_step, 3)
                V.tensor_copy(dump_f[:], dump_i[:]).then_inc(v_small, 1)
                ve.wait_ge(fuse_v, 2)
                for k, (whole, parts) in enumerate(((w23_sb[:], w23_p), (f2_sb, f2_p), (f3_sb, f3_p))):
                    V.tensor_copy(parts[0][:], whole).then_inc(part_ready, 1)
                    ve.wait_ge(part_ready, 2 * k + 1)
                    V.tensor_tensor(parts[1][:], whole, parts[0][:].bitcast(F32), ALU.subtract).then_inc(part_ready, 1)

            node_loop(ve, nodes, 0)
            ve.wait_ge(v_small, 9)
            ve.wait_ge(p_const, 2)
            ve.wait_ge(part_ready, 6)

            def basis(s, q):
                ve.wait_ge(exp_ready, s + 1)
                wait_past(ve, z1_ready, s - 1)
                V.tensor_tensor(r_in[q][:], u[q][:], e_bc[q][:], ALU.mult).then_inc(r_ready, 1)

            def targets(s, n, q):
                ve.wait_ge(src_in[q], 32 * (n + 1))
                wait_past(ve, c_ready, s * 4 - 4)
                sc = src_c[q][:]
                V.tensor_scalar(to_dump[:], sc, -1.0, dump_f[:], ALU.mult, ALU.add).then_inc(dump_ready, 1)
                for j in range(8):
                    i = V.scalar_tensor_tensor(same[q][:, j, :], src_r[q][:, j * P:(j + 1) * P], src_c[q][:, j:j + 1], upto[:],
                                               ALU.is_equal, ALU.mult, accum_out=n_upto[:, j:j + 1])
                i.then_inc(cnt_ready, 1)
                ve.wait_ge(cnt_ready, s + 1)
                ve.wait_ge(dump_ready, s + 1)
                V.scalar_tensor_tensor(is_dup[:], n_upto[:], 1.5, to_dump[:], ALU.is_gt, ALU.mult).then_inc(dup_ready, 1)
                ve.wait_ge(dup_ready, s + 1)
                for i in range(N_TAB):
                    wait_past(ve, scat[i], (s - 1) * (16 * 8 // N_TAB))
                V.tensor_tensor(target[q][:], is_dup[:], sc, ALU.add).then_inc(tgt_ready, 1)

            def rest1(s, q):
                ve.wait_ge(a1_ready, s + 1)
                wait_past(ve, z2_ready, s * 4 - 4)
                V.tensor_tensor(a1_p[q][1][:], a1, a1_p[q][0][:].bitcast(F32), ALU.subtract).then_inc(lo1_ready, 1)

            def rest(c, k, ready, a, a_p, read, done):
                for m in range(2):
                    ve.wait_ge(ready, c * 2 + m + 1)
                    if m == 0:
                        wait_past(ve, read, c * 2 - 2)
                    V.tensor_tensor(a_p[k % 2][1][:, m, :], a[m], a_p[k % 2][0][:, m, :].bitcast(F32),
                                    ALU.subtract).then_inc(done, 1)

            def messages(c, n, k):
                s_half = k % 2
                q = (k % 4) // 2
                n2 = n + (k - k % 4) // 4

                def product(pair):
                    ve.wait_ge(w_ready, c * 2 + pair + 1)
                    ve.wait_ge(gath[q][s_half * 2 + pair], 32 * (n2 + 1))
                    wait_past(ve, c_ready, c * 2 - 3 + pair)
                    V.tensor_tensor(msg[pair][:], wps[pair][:], hn_g[q][s_half * 2 + pair], ALU.mult).then_inc(msg_ready, 1)

                def high(pair):
                    ve.wait_ge(msg_ready, c * 2 + pair + 1)
                    V.tensor_copy(msg_p[s_half][pair][0][:], msg[pair][:]).then_inc(mhi_ready, 1)

                def low(pair):
                    hi, lo = msg_p[s_half][pair]
                    ve.wait_ge(mhi_ready, c * 2 + pair + 1)
                    V.tensor_tensor(lo[:], msg[pair][:], hi[:].bitcast(F32), ALU.subtract).then_inc(mlo_ready, 1)

                product(0)
                high(0)
                product(1)
                low(0)
                high(1)
                low(1)

            def step(t, n, k):
                if exists(t):
                    rest(t, k, a2_ready, a2, a2_p, z3_ready, lo2_ready)
                if k % 2 == 1 and exists(n * 2 + (k + 1) // 2, N_SUPER):
                    rest1(n * 2 + (k + 1) // 2, (k + 1) // 2 % 2)
                if k == 2 and exists(n * 2 + 2, N_SUPER):
                    for i in range(2):
                        basis(n * 2 + 2 + i, i)
                if exists(t - 1):
                    rest(t - 1, k + 1, a3_ready, a3, a3_p, w_ready, lo3_ready)
                if exists(t - 2):
                    messages(t - 2, n, k - 2)
                if k % 2 == 1:
                    s = n * 2 + k // 2
                    if exists(s, N_SUPER):
                        targets(s, n, k // 2)

            for s in range(2):
                basis(s, s)
            rest1(0, 0)
            edge_loop(ve, step, 3)

            ve.wait_ge(bc_in, 16 * N_BC)

            def last(g, n, slot):
                ve.wait_ge(sum_in[slot], 16 * (n + 1))

                def centre(t):
                    i = V.scalar_tensor_tensor(f_t[slot][:, t, :], f_t[slot][:, t, :], st2[slot][:, t, 0:1], lg_bc[:],
                                               ALU.subtract, ALU.mult)
                    if t == G_T - 1:
                        i.then_inc(fc_ready, 1)

                layernorm(slot, f_t[slot], (g + N_GROUPS) * LN_STEPS, centre)
                ve.wait_ge(fc_ready, g + 1)
                wait_past(ve, out_ready, g - 2)
                for t in range(G_T):
                    i = V.scalar_tensor_tensor(f_n[slot][:, t, :], f_t[slot][:, t, :], rstd[slot][:, t:t + 1], lb_bc[:],
                                               ALU.mult, ALU.add)
                i.then_inc(fn_ready, 1)

            node_loop(ve, last, 0)

            n, slot = divmod(N_GROUPS - 1, SLOTS)
            ve.wait_ge(out_ready, N_GROUPS - 1)
            ve.wait_ge(sg_ready, N_GROUPS * 3)
            V.tensor_tensor(f_o[slot], f_o[slot], f_n[slot], ALU.mult).then_inc(fg_ready, 1)
            ve.wait_ge(fx_in[slot], 16 * (n + 1))
            ve.wait_ge(fg_ready, N_GROUPS)
            V.tensor_tensor(f_o[slot], f_o[slot], f_x[slot], ALU.add).then_inc(out_ready, 1)


_INS = ["x", "src_cols", "src_rows", "dst_cols", "dist", "centers", "widths", "w1", "b1", "w2t", "b2", "f1", "fb1",
        "f2", "fb2", "f3", "fb3", "node_w", "node_b", "ln_g", "ln_b", "gate_w", "gate_b"]


def kernel(x, src, dst, edge_weight, L0_gnn_centers, L0_gnn_widths, L0_gnn_rbf_w1, L0_gnn_rbf_b1,
           L0_gnn_rbf_w2, L0_gnn_rbf_b2, L0_gnn_filt_w1, L0_gnn_filt_b1, L0_gnn_filt_w2, L0_gnn_filt_b2,
           L0_gnn_filt_w3, L0_gnn_filt_b3, L0_gnn_node_w, L0_gnn_node_b, L0_gnn_ln_g, L0_gnn_ln_b,
           L0_gnn_gate_w, L0_gnn_gate_b):
    import concourse.bacc as bacc
    from concourse.bass_utils import run_bass_kernel_spmd

    def pad(a, n, value=0):
        a = np.asarray(a)
        return np.concatenate([a, np.full((n - a.shape[0],) + a.shape[1:], value, a.dtype)])

    def columns(a):
        return np.ascontiguousarray(a.reshape(N_SUPER, 8, TILE).transpose(0, 2, 1))

    def halves(a):
        return np.ascontiguousarray(np.asarray(a).reshape(2, P).T)

    src_p = pad(src, E_PAD, N_PAD - 1)
    dst_p = pad(dst, E_PAD, 0)
    w2t = np.asarray(L0_gnn_rbf_w2).T
    arrays = {
        "x": pad(x, N_PAD), "src_cols": columns(src_p), "src_rows": src_p, "dst_cols": columns(dst_p),
        "dist": pad(edge_weight, E_PAD), "centers": L0_gnn_centers,
        "widths": np.concatenate([np.asarray(L0_gnn_widths)] * 2).reshape(P, 1),
        "w1": L0_gnn_rbf_w1, "b1": L0_gnn_rbf_b1, "w2t": np.concatenate([w2t, w2t], axis=1), "b2": L0_gnn_rbf_b2,
        "f1": L0_gnn_filt_w1, "fb1": halves(L0_gnn_filt_b1), "f2": L0_gnn_filt_w2, "fb2": halves(L0_gnn_filt_b2),
        "f3": L0_gnn_filt_w3, "fb3": L0_gnn_filt_b3, "node_w": L0_gnn_node_w, "node_b": L0_gnn_node_b,
        "ln_g": L0_gnn_ln_g, "ln_b": L0_gnn_ln_b, "gate_w": L0_gnn_gate_w, "gate_b": L0_gnn_gate_b,
    }
    arrays = {k: np.ascontiguousarray(v) for k, v in arrays.items()}
    nc = bacc.Bacc("TRN2", target_bir_lowering=False, num_devices=1)
    args = [nc.dram_tensor(n, arrays[n].shape, mybir.dt.from_np(arrays[n].dtype), kind="ExternalInput").ap() for n in _INS]
    args.append(nc.dram_tensor("out", (N_PAD, HID), F32, kind="ExternalOutput").ap())
    build(nc, *args)
    result = run_bass_kernel_spmd(nc, [arrays], core_ids=[0])
    return result.results[0]["out"][:N_NODES]
```
